# Optimizing a Trainium2 kernel written in Bass

```python
import numpy as np
import jax
import jax.numpy as jnp

def _softmax(x, axis=-1):
    return jax.nn.softmax(x, axis=axis)

def _gelu(x):
    return jax.nn.gelu(x, approximate=True)

def _silu(x):
    return jax.nn.silu(x)

def _sigmoid(x):
    return jax.nn.sigmoid(x)

def _layernorm(x, axis=-1, eps=1e-05):
    m = jnp.mean(x, axis=axis, keepdims=True)
    v = jnp.var(x, axis=axis, keepdims=True)
    return (x - m) / jnp.sqrt(v + eps)

def _scatter_add(tgt, idx, src, axis=0):
    return tgt.at[idx].add(src)

def _segment_sum(src, seg, n):
    return jax.ops.segment_sum(src, seg, n)
kernel_name = 'mk_cond_resid_d1_seqx_r2_44c137'

def setup_inputs(seed: int=0):
    np.random.seed(seed)
    _w = jnp.asarray

    def _rec_inputs():
        import jax
        import jax.numpy as jnp
        _rk = jax.random.key(seed)
        x = 7.22e-05 + 1 * jax.random.normal(jax.random.fold_in(_rk, 1), (8, 512, 512), jnp.float32)
        _lenS = 512 - jax.random.randint(jax.random.fold_in(_rk, 7), (8,), 0, max(1, 512 // 4) + 1, jnp.int32)
        _lenS2 = 512 - jax.random.randint(jax.random.fold_in(_rk, 8), (8,), 0, max(1, 512 // 4) + 1, jnp.int32)
        cond_64 = -0.104238 + 1.01173 * jax.random.normal(jax.random.fold_in(_rk, 11), (8, 64), jnp.float32)
        return (x, cond_64)
    x, cond_64 = _rec_inputs()

    def _L0_cond_setup():
        import jax, jax.numpy as jnp
        import numpy as np
        B, S, H = (4, 1024, 512)
        E = 8
        M = 256
        K = 2
        N_SHARED = 2
        SM = M * N_SHARED
        G = 64
        GE_TEMP = 1.0
        ALPHA = 0.001
        SEQ_AUX = True
        NORM_TOPK = True
        COS_TEMP = 0.78
        CONS_ALPHA = 0.01
        LEAKY_SLOPE = 0.01
        EPS_COS = 1e-08

        def _leaky(x):
            return jnp.where(x >= 0, x, LEAKY_SLOPE * x)

        def _moe_forward(hidden_states, g, wt, wg, w_gate, w_up, w_down, sw_gate, sw_up, sw_down):
            b, s, h = hidden_states.shape
            x = hidden_states.reshape(-1, h)
            T = x.shape[0]
            logits_h = x @ wt.T
            logits_g = g @ wg.T
            logits_g = jnp.repeat(logits_g, s, axis=0)
            logits = (logits_h + logits_g / GE_TEMP) / (1.0 + 1.0 / GE_TEMP)
            scores = jax.nn.softmax(logits, axis=-1)
            topk_w, topk_idx = jax.lax.top_k(scores, K)
            if K > 1 and NORM_TOPK:
                topk_w = topk_w / (topk_w.sum(-1, keepdims=True) + 1e-20)
            onehot = jax.nn.one_hot(topk_idx.reshape(b, s * K), E, dtype=jnp.float32)
            ce = onehot.sum(1) / (s * K / E)
            aux_loss = (ce * scores.reshape(b, s, E).mean(1)).sum(1).mean() * ALPHA
            gp = _leaky(jnp.einsum('th,ehm->etm', x, w_gate))
            up = jnp.einsum('th,ehm->etm', x, w_up)
            y_all = jnp.einsum('etm,emh->eth', gp * up, w_down)
            y_sel = y_all[topk_idx, jnp.arange(T)[:, None], :]
            y = (y_sel * topk_w[..., None]).sum(1).reshape(b, s, h)
            p = _leaky(hidden_states @ sw_gate) * (hidden_states @ sw_up) @ sw_down
            y = y + p
            num = jnp.sum(y * p, -1)
            den = jnp.maximum(jnp.linalg.norm(y, axis=-1), EPS_COS) * jnp.maximum(jnp.linalg.norm(p, axis=-1), EPS_COS)
            closs = CONS_ALPHA * jnp.mean(num / den / (1.0 + COS_TEMP))
            return (y, aux_loss + closs)
        key = jax.random.key(seed)
        ks = jax.random.split(key, 12)
        sh = 1.0 / np.sqrt(H)
        sm = 1.0 / np.sqrt(M)
        ssm = 1.0 / np.sqrt(SM)
        sg = 1.0 / np.sqrt(G)
        return {'hidden_states': jax.random.normal(ks[0], (B, S, H), jnp.float32), 'g': jax.random.normal(ks[1], (B, G), jnp.float32), 'wt': jax.random.uniform(ks[2], (E, H), jnp.float32, -sh, sh), 'wg': jax.random.uniform(ks[3], (E, G), jnp.float32, -sg, sg), 'w_gate': jax.random.uniform(ks[4], (E, H, M), jnp.float32, -sh, sh), 'w_up': jax.random.uniform(ks[5], (E, H, M), jnp.float32, -sh, sh), 'w_down': jax.random.uniform(ks[6], (E, M, H), jnp.float32, -sm, sm), 'sw_gate': jax.random.uniform(ks[7], (H, SM), jnp.float32, -sh, sh), 'sw_up': jax.random.uniform(ks[8], (H, SM), jnp.float32, -sh, sh), 'sw_down': jax.random.uniform(ks[9], (SM, H), jnp.float32, -ssm, ssm)}
    _L0_cond_all = _L0_cond_setup()
    _L0_cond_in = {k: v for k, v in _L0_cond_all.items() if k in ('wt', 'wg', 'w_gate', 'w_up', 'w_down', 'sw_gate', 'sw_up', 'sw_down')}
    del _L0_cond_all
    return {'x': x, 'cond_64': cond_64, 'L0_cond_wt': _L0_cond_in['wt'], 'L0_cond_wg': _L0_cond_in['wg'], 'L0_cond_w_gate': _L0_cond_in['w_gate'], 'L0_cond_w_up': _L0_cond_in['w_up'], 'L0_cond_w_down': _L0_cond_in['w_down'], 'L0_cond_sw_gate': _L0_cond_in['sw_gate'], 'L0_cond_sw_up': _L0_cond_in['sw_up'], 'L0_cond_sw_down': _L0_cond_in['sw_down']}

def reference(x, cond_64, L0_cond_wt, L0_cond_wg, L0_cond_w_gate, L0_cond_w_up, L0_cond_w_down, L0_cond_sw_gate, L0_cond_sw_up, L0_cond_sw_down):
    import jax
    import jax.numpy as jnp

    def _L0_cond_ref(hidden_states, g, wt, wg, w_gate, w_up, w_down, sw_gate, sw_up, sw_down):
        import jax, jax.numpy as jnp
        import numpy as np
        B, S, H = (4, 1024, 512)
        E = 8
        M = 256
        K = 2
        N_SHARED = 2
        SM = M * N_SHARED
        G = 64
        GE_TEMP = 1.0
        ALPHA = 0.001
        SEQ_AUX = True
        NORM_TOPK = True
        COS_TEMP = 0.78
        CONS_ALPHA = 0.01
        LEAKY_SLOPE = 0.01
        EPS_COS = 1e-08

        def _leaky(x):
            return jnp.where(x >= 0, x, LEAKY_SLOPE * x)

        def _moe_forward(hidden_states, g, wt, wg, w_gate, w_up, w_down, sw_gate, sw_up, sw_down):
            b, s, h = hidden_states.shape
            x = hidden_states.reshape(-1, h)
            T = x.shape[0]
            logits_h = x @ wt.T
            logits_g = g @ wg.T
            logits_g = jnp.repeat(logits_g, s, axis=0)
            logits = (logits_h + logits_g / GE_TEMP) / (1.0 + 1.0 / GE_TEMP)
            scores = jax.nn.softmax(logits, axis=-1)
            topk_w, topk_idx = jax.lax.top_k(scores, K)
            if K > 1 and NORM_TOPK:
                topk_w = topk_w / (topk_w.sum(-1, keepdims=True) + 1e-20)
            onehot = jax.nn.one_hot(topk_idx.reshape(b, s * K), E, dtype=jnp.float32)
            ce = onehot.sum(1) / (s * K / E)
            aux_loss = (ce * scores.reshape(b, s, E).mean(1)).sum(1).mean() * ALPHA
            gp = _leaky(jnp.einsum('th,ehm->etm', x, w_gate))
            up = jnp.einsum('th,ehm->etm', x, w_up)
            y_all = jnp.einsum('etm,emh->eth', gp * up, w_down)
            y_sel = y_all[topk_idx, jnp.arange(T)[:, None], :]
            y = (y_sel * topk_w[..., None]).sum(1).reshape(b, s, h)
            p = _leaky(hidden_states @ sw_gate) * (hidden_states @ sw_up) @ sw_down
            y = y + p
            num = jnp.sum(y * p, -1)
            den = jnp.maximum(jnp.linalg.norm(y, axis=-1), EPS_COS) * jnp.maximum(jnp.linalg.norm(p, axis=-1), EPS_COS)
            closs = CONS_ALPHA * jnp.mean(num / den / (1.0 + COS_TEMP))
            return (y, aux_loss + closs)
        y, _ = _moe_forward(hidden_states, g, wt, wg, w_gate, w_up, w_down, sw_gate, sw_up, sw_down)
        return y
    x = x + _L0_cond_ref(x, cond_64, L0_cond_wt, L0_cond_wg, L0_cond_w_gate, L0_cond_w_up, L0_cond_w_down, L0_cond_sw_gate, L0_cond_sw_up, L0_cond_sw_down)
    return x

_drawn_inputs = setup_inputs


def setup_inputs(seed=0):
    import zlib

    import numpy as np

    out = dict(_drawn_inputs(seed))
    spreads = {}
    factors = {}
    for name, (base, spread) in spreads.items():
        noise = np.random.default_rng([zlib.crc32(name.encode()), seed]).standard_normal(out[name].shape)
        drawn = base * np.exp(spread * noise) if base else spread * noise
        out[name] = jnp.asarray(drawn.astype(out[name].dtype))
    for name, factor in factors.items():
        out[name] = (out[name] * factor).astype(out[name].dtype)
    return out
```

```python
import concourse.bass as bass
from concourse import mybir
from contextlib import ExitStack

P = 128
T, H, NE, M, SM, G = 4096, 512, 8, 256, 512, 64
KH = H // P
KM = M // P
KS = SM // P
TOPK = 2
GT = 512
NG = T // GT
TPG = GT // P
NC = T // P
U = 4
TILES = -(-(T * TOPK // P + NE - 1) // U) * U
SLOPE = 0.01
C_ID, C_TRI, C_IOTA, C_REV, C_SCAN, C_P, C_TOK, C_W = 0, 128, 256, 384, 392, 648, 649, 681


def moe_kernel(nc, x, xT, wtT, wgT, condT, w_gate, w_up, w_down, sw_gate, sw_up, sw_down, consts, out):
    F32, BF16, I32 = mybir.dt.float32, mybir.dt.bfloat16, mybir.dt.int32
    ALU, ACT, AX = mybir.AluOpType, mybir.ActivationFunctionType, mybir.AxisListType

    xT_v = xT.rearrange("(k p) t -> p k t", p=P)
    wtT_v = wtT.rearrange("(k p) e -> p k e", p=P)
    ctx = ExitStack()
    with ctx:
        def sb(name, shape, dt=F32):
            return ctx.enter_context(nc.sbuf_tensor(name, shape, dt))

        def sem(name):
            return ctx.enter_context(nc.semaphore(name))

        def sems(name, n):
            return [sem(f"{name}{i}") for i in range(n)]

        slot_rows = nc.dram_tensor("slot_rows", (TILES * P, H), F32, kind="Internal").ap()

        wgu = sb("wgu", [P, NE, KH, 2 * M])
        wdn = sb("wdn", [P, NE, KM, H])
        swg = sb("swg", [P, KH, SM])
        swu = sb("swu", [P, KH, SM])
        swd = sb("swd", [P, KS, H])
        cst = sb("cst", [P, C_W])
        tri = sb("tri", [P, P], BF16)
        ones = sb("ones", [P, P], BF16)
        wt_sb = sb("wt_sb", [P, KH, NE])
        wg_sb = sb("wg_sb", [G, NE])
        cond_sb = sb("cond_sb", [G, NG])
        bias_sb = sb("bias_sb", [NE, NG])
        pos = sb("pos", [P, TOPK, NC], I32)
        wts = sb("wts", [P, TOPK, NC])
        slot_tok = sb("slot_tok", [P, TILES], I32)
        tile_exp = sb("tile_exp", [1, TILES], I32)
        idx_e = sb("idx_e", [P, U], I32)
        idx_c = sb("idx_c", [P, U, TOPK], I32)
        xt = sb("xt", [P, 2, KH, GT])
        area = sb("area", [P, 4096])
        ht = area[:, 0:2048].rearrange("p (m t) -> p m t", m=KS)
        gs = area[:, 2048:3072].rearrange("p (b t) -> p b t", b=2)
        lg = area[:, 3072:4096].rearrange("p (b t) -> p b t", b=2)
        xts = area[:, 0:1024].rearrange("p (b c) -> p b c", b=2)
        ge = area[:, 1024:1536].rearrange("p (b m) -> p b m", b=2)
        lge = area[:, 1536:2048].rearrange("p (b m) -> p b m", b=2)
        he = area[:, 2048:2560].rearrange("p (b m) -> p b m", b=2)
        hts = area[:, 2560:3072].rearrange("p (b m) -> p b m", b=2)
        xg = sb("xg", [P, U, H])
        late = sb("late", [P, 9216])
        acc = late[:, 0:4096].rearrange("p (s h) -> p s h", s=2 * TPG)
        yg = late[:, 4096:6144].rearrange("p (b k h) -> p b k h", b=2, k=TOPK)
        ysb = late[:, 6144:8192].rearrange("p (b h) -> p b h", b=U)
        xrow = late[:, 8192:9216].rearrange("p (b h) -> p b h", b=2)
        hot_row = late[:, 0:4096].bitcast(BF16).rearrange("p (k c r) -> p k c r", k=TOPK, c=NC)
        hw = TILES * NC // 2
        hot_p = [late[:, 4096 + k * hw:4096 + (k + 1) * hw].bitcast(BF16).rearrange("p (c t) -> p c t", c=NC)
                 for k in range(TOPK)]
        hot_c = [late[:, 4096 + (2 + k) * hw:4096 + (3 + k) * hw].bitcast(BF16).rearrange("p (c t) -> p c t", c=NC)
                 for k in range(TOPK)]
        lt = xg[0:NE, 0:2, :]
        scr = xt[:, 1, :, :].rearrange("p k t -> p (k t)")

        def s3(i):
            return scr[:, i * 256:(i + 1) * 256].rearrange("p (c e) -> p c e", e=NE)

        logit, prob, keep, eq = s3(0), s3(1), s3(2), s3(3)
        hot1, hot2, rank, tmp = s3(4), s3(5), s3(6), s3(7)
        small = sb("small", [P, 12, NC])
        member = sb("member", [P, NC, NE], BF16)
        cnt_ec = xg[:, 2, 0:NE * NC].rearrange("p (e c) -> p e c", e=NE)
        cum_ec = xg[:, 3, 0:NE * NC].rearrange("p (e c) -> p e c", e=NE)
        etmp = sb("etmp", [P, 6, NE])
        eint = sb("eint", [P, NE], I32)
        cmp_te = sb("cmp_te", [1, TILES, NE])
        tile_f = sb("tile_f", [1, TILES])
        row_i = sb("row_i", [P, 2 * TOPK, NC], I32)
        row_f = sb("row_f", [P, 2 * TOPK, NC])

        bank = [ctx.enter_context(nc.psum_tensor(f"bank{i}", [P, 512], F32)) for i in range(8)]
        ps_g, ps_u, ps_p = bank[0:2], bank[2:4], bank[6:8]
        ps_x, ps_gu, ps_h, ps_y = bank[0:2], bank[2:4], bank[4:6], bank[6:8]
        ps_lt, ps_bias, ps_log, ps_rank, ps_cnt, ps_map = bank[6:8], bank[4], bank[5], bank[4], bank[3], bank[4]

        cst_in = sem("cst_in")
        xt_in = sems("xt_in", 2)
        sw_in = sem("sw_in")
        ew_in = sem("ew_in")
        x_in = sems("x_in", 2)
        cast = sem("cast")
        bias_mm, bias_ok = sem("bias_mm"), sem("bias_ok")
        lt_mm, lt_ok, log_tr = sem("lt_mm"), sem("lt_ok"), sem("log_tr")
        r_step = sem("r_step")
        exp_in, exp_ok = sem("exp_in"), sem("exp_ok")
        member_ok, rank_mm, rowtile_ok, route_ok = sem("member_ok"), sem("rank_mm"), sem("rowtile_ok"), sem("route_ok")
        hots_ok, map_mm, map_ok = sem("hots_ok"), sem("map_mm"), sem("map_ok")
        gu_mm, gs_ok, lg_ok, h_ok = sem("gu_mm"), sem("gs_ok"), sem("lg_ok"), sem("h_ok")
        p_mm, acc_ok = sem("p_mm"), sem("acc_ok")
        eidx_ok, xg_in = sem("eidx_ok"), sems("xg_in", U)
        ex_tr, ex_ok, eg_mm, eg_ok, elg_ok, eh_ok = (sem("ex_tr"), sem("ex_ok"), sem("eg_mm"), sem("eg_ok"),
                                                     sem("elg_ok"), sem("eh_ok"))
        eh_tr, eht_ok, ey_mm, ey_ok, y_out = sem("eh_tr"), sem("eht_ok"), sem("ey_mm"), sem("ey_ok"), sems("y_out", U)
        cidx_ok, yg_in = sem("cidx_ok"), sems("yg_in", 2)
        half_ok, comb_ok, out_st = sem("half_ok"), sem("comb_ok"), sems("out_st", 2 * TPG)

        block = ctx.enter_context(nc.Block())
        order = list(range(1, NG)) + [0]

        @block.sync
        def _(sp):
            sp.dma_start(cst[:, :], consts).then_inc(cst_in, 16)
            sp.dma_start(wt_sb[:, :, :], wtT_v).then_inc(cst_in, 16)
            sp.dma_start(wg_sb[:, :], wgT).then_inc(cst_in, 16)
            sp.dma_start(cond_sb[:, :], condT).then_inc(cst_in, 16)
            for j, g in enumerate(order):
                if j >= 2:
                    sp.wait_ge(lt_mm, j - 1)
                sp.dma_start(xt[:, g % 2, :, :], xT_v[:, :, g * GT:(g + 1) * GT]).then_inc(xt_in[g % 2], 16)
            for dst, src in ((swg, sw_gate), (swu, sw_up), (swd, sw_down)):
                sp.dma_start(dst[:, :, :], src.rearrange("(k p) n -> p k n", p=P)).then_inc(sw_in, 16)
            for e in range(NE):
                sp.dma_start(wgu[:, e, :, 0:M], w_gate[e].rearrange("(k p) n -> p k n", p=P)).then_inc(ew_in, 16)
                sp.dma_start(wgu[:, e, :, M:2 * M], w_up[e].rearrange("(k p) n -> p k n", p=P)).then_inc(ew_in, 16)
                sp.dma_start(wdn[:, e, :, :], w_down[e].rearrange("(k p) n -> p k n", p=P)).then_inc(ew_in, 16)

            def load_xrow(g, t):
                sp.dma_start(xrow[:, t % 2, :], x[bass.ds((g * TPG + t) * P, P), :]).then_inc(x_in[t % 2], 16)

            sp.wait_ge(map_mm, 1)
            for t in range(TPG):
                if t >= 2:
                    sp.wait_ge(acc_ok, t - 1)
                load_xrow(0, t)
            sp.wait_ge(route_ok, 1)
            sp.dma_start(xt[:, 1, :, :], xT_v[:, :, GT:2 * GT]).then_inc(xt_in[1], 16)
            with sp.Fori(0, TILES // U) as j:
                for b in range(U):
                    sp.wait_ge(ey_ok, j * U + (b + 1))
                    sp.dma_start(slot_rows[bass.ds((j * U + b) * P, P), :], ysb[:, b, :]).then_inc(y_out[b], 16)

            def store(g, t, par):
                sp.wait_ge(comb_ok, g * TPG + (t + 1))
                sp.dma_start(out[bass.ds((g * TPG + t) * P, P), :],
                             acc[:, par * TPG + t, :]).then_inc(out_st[par * TPG + t], 16)

            def group(g, par, last=False):
                if not last:
                    sp.wait_ge(gu_mm, g * KS)
                    sp.dma_start(xt[:, 1 - par, :, :],
                                 xT_v[:, :, bass.ds(g * GT + GT, GT)]).then_inc(xt_in[1 - par], 16)
                for t in range(2):
                    sp.wait_ge(acc_ok, g * TPG + (t - 1))
                    load_xrow(g, t)
                for t in range(TPG):
                    store(g - 1, t, 1 - par)
                for t in range(2, TPG):
                    sp.wait_ge(acc_ok, g * TPG + (t - 1))
                    load_xrow(g, t)

            with sp.Fori(0, (NG - 2) // 2) as j:
                group(j * 2 + 1, 1)
                group(j * 2 + 2, 0)
            group(NG - 1, 1, last=True)
            for t in range(TPG):
                store(NG - 1, t, 1)
            for par in range(2):
                for t in range(TPG):
                    sp.wait_ge(out_st[par * TPG + t], 16 * (NG // 2))

        @block.gpsimd
        def _(pool):
            def index_x(i, b):
                nc.gpsimd.tensor_copy(idx_e[:, b:b + 1], slot_tok[:, bass.ds(i, 1)]).then_inc(eidx_ok, 1)

            def gather_x(b):
                nc.gpsimd.indirect_dma_start(out=xg[:, b, :], out_offset=None, in_=x,
                                             in_offset=bass.IndirectOffsetOnAxis(ap=idx_e[:, b:b + 1], axis=0)
                                             ).then_inc(xg_in[b], 16)

            def turn_x(j, b):
                i = j * U + b
                pool.wait_ge(ex_tr, i - (U - 2))
                pool.wait_ge(eidx_ok, i + 1)
                index_x(i + 1, (b + 1) % U)
                gather_x(b)

            pool.wait_ge(map_ok, 1)
            index_x(0, 0)
            for b in range(U - 1):
                pool.wait_ge(eidx_ok, b + 1)
                index_x(b + 1, b + 1)
                gather_x(b)
            turn_x(0, U - 1)
            with pool.Fori(1, TILES // U - 1) as j:
                for b in range(U):
                    turn_x(j, b)
            for b in range(U - 1):
                turn_x(TILES // U - 1, b)
            pool.wait_ge(ex_tr, TILES - U)
            pool.wait_ge(eidx_ok, TILES)
            gather_x(U - 1)

            def index_y(c, b):
                nc.gpsimd.tensor_copy(idx_c[:, b, :], pos[:, :, bass.ds(c, 1)].rearrange("p k o -> p (k o)")).then_inc(cidx_ok, 1)

            def gather_y(b):
                for k in range(TOPK):
                    nc.gpsimd.indirect_dma_start(out=yg[:, b % 2, k, :], out_offset=None, in_=slot_rows,
                                                 in_offset=bass.IndirectOffsetOnAxis(ap=idx_c[:, b, k:k + 1], axis=0)
                                                 ).then_inc(yg_in[b % 2], 16)

            def turn_y(j, b):
                c = j * U + b
                pool.wait_ge(comb_ok, c - 1)
                pool.wait_ge(cidx_ok, c + 1)
                index_y(c + 1, (b + 1) % U)
                gather_y(b)

            index_y(0, 0)
            for b in range(U):
                pool.wait_ge(y_out[b], 16 * (TILES // U))
            for b in range(2):
                pool.wait_ge(cidx_ok, b + 1)
                index_y(b + 1, b + 1)
                gather_y(b)
            for b in range(2, U):
                turn_y(0, b)
            with pool.Fori(1, NC // U - 1) as j:
                for b in range(U):
                    turn_y(j, b)
            for b in range(U - 1):
                turn_y(NC // U - 1, b)
            pool.wait_ge(comb_ok, NC - 2)
            pool.wait_ge(cidx_ok, NC)
            gather_y(U - 1)

        @block.scalar
        def _(act):
            act.wait_ge(cst_in, 64)
            nc.scalar.copy(tri[:, :], cst[:, C_TRI:C_TRI + P])
            nc.scalar.activation(ones[:, :], cst[:, C_TRI:C_TRI + P], ACT.Copy, bias=1.0, scale=0.0).then_inc(cast, 1)
            act.wait_ge(exp_in, 1)
            nc.scalar.activation(prob, keep, ACT.Exp).then_inc(exp_ok, 1)

            def shared_gate(s, b, wait_free=True):
                act.wait_ge(gu_mm, s + 1)
                if wait_free:
                    act.wait_ge(h_ok, s - 1)
                nc.scalar.copy(gs[:, b, :], ps_g[b][:, :]).then_inc(gs_ok, 1)

            for m in range(KS):
                shared_gate(m, m % 2, wait_free=m >= 2)

            def x_out(i, b):
                act.wait_ge(ex_tr, i + 1)
                nc.scalar.copy(xts[:, b, :], ps_x[b][:, :]).then_inc(ex_ok, 1)

            def gate_out(i, b):
                act.wait_ge(eg_mm, i + 1)
                nc.scalar.copy(ge[:, b, :], ps_gu[b][:, 0:M]).then_inc(eg_ok, 1)

            def y_rows(i, b, b4, stored):
                act.wait_ge(ey_mm, i + 1)
                if stored is not None:
                    act.wait_ge(y_out[b4], stored)
                nc.scalar.copy(ysb[:, b4, :], ps_y[b][:, :]).then_inc(ey_ok, 1)

            def turn(j, last=False):
                for b in range(U):
                    i = j * U + b
                    gate_out(i, b % 2)
                    if not (last and b == U - 1):
                        x_out(i + 1, (b + 1) % 2)
                    if b > 0:
                        y_rows(i - 1, (b - 1) % 2, b - 1, None if isinstance(j, int) and j == 0 else j * 16)
                    elif not (isinstance(j, int) and j == 0):
                        y_rows(i - 1, 1, U - 1, None if isinstance(j, int) and j == 1 else j * 16 - 16)

            act.wait_ge(acc_ok, TPG)
            x_out(0, 0)
            turn(0)
            turn(1)
            with act.Fori(2, TILES // U - 1) as j:
                turn(j)
            turn(TILES // U - 1, last=True)
            y_rows(TILES - 1, 1, U - 1, 16 * (TILES // U - 1))

            with act.Fori(1, NG) as g:
                for m in range(KS):
                    shared_gate(g * KS + m, m % 2)

        @block.vector
        def _(dve):
            step = [0]

            def then(ins):
                step[0] += 1
                ins.then_inc(r_step, 1)
                dve.wait_ge(r_step, step[0])

            def bc(v):
                return v.unsqueeze(2).to_broadcast([P, NC, NE])

            V = nc.vector
            dve.wait_ge(cst_in, 64)
            dve.wait_ge(bias_mm, 1)
            V.tensor_copy(bias_sb[:, :], ps_bias[0:NE, 0:NG]).then_inc(bias_ok, 1)
            dve.wait_ge(bias_ok, 1)
            for j, g in enumerate(order):
                dve.wait_ge(lt_mm, j + 1)
                if j >= 2:
                    dve.wait_ge(log_tr, j - 1)
                V.tensor_scalar(lt[:, j % 2, :], ps_lt[j % 2][0:NE, :], bias_sb[:, g:g + 1], 0.5,
                                ALU.add, ALU.mult).then_inc(lt_ok, 1)
            dve.wait_ge(log_tr, NG)
            mx, den, m1, m2, r1, r2, wsum = (small[:, i] for i in range(7))
            then(V.tensor_copy(logit, ps_log[:, 0:NC * NE].rearrange("p (c e) -> p c e", e=NE)))
            then(V.tensor_reduce(mx, logit, AX.X, ALU.max))
            V.tensor_tensor(keep, logit, bc(mx), ALU.subtract).then_inc(exp_in, 1)
            dve.wait_ge(exp_ok, 1)
            then(V.tensor_reduce(den, prob, AX.X, ALU.add))
            then(V.reciprocal(den, den))
            then(V.tensor_tensor(prob, prob, bc(den), ALU.mult))
            rev = cst[:, C_REV:C_REV + NE].unsqueeze(1).to_broadcast([P, NC, NE])
            then(V.tensor_reduce(m1, prob, AX.X, ALU.max))
            then(V.tensor_tensor(eq, prob, bc(m1), ALU.is_equal))
            then(V.tensor_tensor(eq, eq, rev, ALU.mult))
            then(V.tensor_reduce(r1, eq, AX.X, ALU.max))
            then(V.tensor_tensor(hot1, rev, bc(r1), ALU.is_equal))
            then(V.scalar_tensor_tensor(keep, hot1, -2.0, prob, ALU.mult, ALU.add))
            then(V.tensor_reduce(m2, keep, AX.X, ALU.max))
            then(V.tensor_tensor(eq, keep, bc(m2), ALU.is_equal))
            then(V.tensor_tensor(eq, eq, rev, ALU.mult))
            then(V.tensor_reduce(r2, eq, AX.X, ALU.max))
            then(V.tensor_tensor(hot2, rev, bc(r2), ALU.is_equal))
            V.tensor_tensor(member[:, :, :], hot1, hot2, ALU.add).then_inc(member_ok, 1)
            then(V.tensor_tensor(wsum, m1, m2, ALU.add))
            then(V.tensor_scalar(wsum, wsum, 1e-20, None, ALU.add))
            then(V.reciprocal(wsum, wsum))
            V.tensor_tensor(wts[:, 0, :], m1, wsum, ALU.mult)
            V.tensor_tensor(wts[:, 1, :], m2, wsum, ALU.mult)
            dve.wait_ge(rank_mm, 1)
            V.tensor_copy(rank, ps_rank[:, 0:NC * NE].rearrange("p (c e) -> p c e", e=NE))
            then(V.tensor_copy(cnt_ec, ps_cnt[:, 0:NC * NE].rearrange("p (c e) -> p e c", e=NE)))
            cnt_f = cnt_ec.rearrange("p e c -> p (e c)")
            cum_f = cum_ec.rearrange("p e c -> p (e c)")
            then(V.tensor_tensor_scan(cum_f, cst[:, C_SCAN:C_SCAN + NE * NC], cnt_f, 0.0, ALU.mult, ALU.add))
            then(V.tensor_tensor(cnt_ec, cum_ec, cnt_ec, ALU.subtract))
            then(V.tensor_tensor(rank, rank, cnt_ec.rearrange("p e c -> p c e"), ALU.add))
            tot, tiles, end, base, one = (etmp[:, i] for i in range(5))
            then(V.tensor_scalar(tot, cum_ec[:, :, NC - 1], float(P - 1), None, ALU.add))
            then(V.tensor_copy(eint[:, :], tot))
            then(V.tensor_scalar(eint[:, :], eint[:, :], 7, None, ALU.logical_shift_right))
            then(V.tensor_copy(tiles, eint[:, :]))
            then(V.memset(one, 1.0))
            then(V.tensor_tensor_scan(end, one, tiles, 0.0, ALU.mult, ALU.add))
            then(V.tensor_tensor(base, end, tiles, ALU.subtract))
            then(V.tensor_scalar(base, base, float(P), None, ALU.mult))
            then(V.tensor_tensor(rank, rank, base.unsqueeze(1).to_broadcast([P, NC, NE]), ALU.add))
            for k, hot in enumerate((hot1, hot2)):
                then(V.tensor_tensor(tmp, hot, rank, ALU.mult))
                then(V.tensor_reduce(small[:, 8 + k], tmp, AX.X, ALU.add))
            then(V.tensor_copy(pos[:, :, :], small[:, 8:10, :]))
            V.tensor_scalar(row_i[:, 0:TOPK, :], pos[:, :, :], P - 1, None, ALU.bitwise_and)
            then(V.tensor_scalar(row_i[:, TOPK:2 * TOPK, :], pos[:, :, :], 7, None, ALU.logical_shift_right))
            V.tensor_copy(row_f[:, :, :], row_i[:, :, :]).then_inc(rowtile_ok, 1)
            then(V.tensor_tensor(cmp_te[:, :, :], end[0:1].unsqueeze(1).to_broadcast([1, TILES, NE]),
                                 cst[0:1, C_IOTA:C_IOTA + TILES].unsqueeze(2).to_broadcast([1, TILES, NE]), ALU.is_le))
            then(V.tensor_reduce(tile_f[:, :], cmp_te[:, :, :], AX.X, ALU.add))
            V.tensor_scalar(tile_exp[:, :], tile_f[:, :], float(NE - 1), None, ALU.min).then_inc(route_ok, 1)

            def shared_h(s, m):
                b = m % 2
                dve.wait_ge(gs_ok, s + 1)
                V.scalar_tensor_tensor(lg[:, b, :], gs[:, b, :], SLOPE, gs[:, b, :], ALU.mult, ALU.max).then_inc(lg_ok, 1)
                dve.wait_ge(lg_ok, s + 1)
                V.tensor_tensor(ht[:, m, :], lg[:, b, :], ps_u[b][:, :], ALU.mult).then_inc(h_ok, 1)

            def add_x(g, t, par, x_count):
                dve.wait_ge(p_mm, g * TPG + (t + 1))
                dve.wait_ge(x_in[t % 2], x_count)
                V.tensor_tensor(acc[:, par * TPG + t, :], ps_p[t % 2][:, :], xrow[:, t % 2, :],
                                ALU.add).then_inc(acc_ok, 1)

            def combine(g, t, par):
                c = g * TPG + t
                b = t % 2
                a = acc[:, par * TPG + t, :]
                dve.wait_ge(yg_in[b], (g * (TPG // 2) + (t // 2 + 1)) * 32)
                V.scalar_tensor_tensor(a, yg[:, b, 0, :], wts[:, 0, bass.ds(c, 1)], a, ALU.mult, ALU.add).then_inc(half_ok, 1)
                dve.wait_ge(half_ok, c + 1)
                V.scalar_tensor_tensor(a, yg[:, b, 1, :], wts[:, 1, bass.ds(c, 1)], a, ALU.mult, ALU.add).then_inc(comb_ok, 1)

            def hots(k):
                V.tensor_tensor(hot_row[:, k], cst[:, C_IOTA:C_IOTA + P].unsqueeze(1).to_broadcast([P, NC, P]),
                                row_f[:, k].unsqueeze(2).to_broadcast([P, NC, P]), ALU.is_equal).then_inc(hots_ok, 1)
                then(V.tensor_tensor(hot_p[k], cst[:, C_IOTA:C_IOTA + TILES].unsqueeze(1).to_broadcast([P, NC, TILES]),
                                     row_f[:, TOPK + k].unsqueeze(2).to_broadcast([P, NC, TILES]), ALU.is_equal))
                then(V.tensor_tensor(hot_c[k], hot_p[k],
                                     cst[:, C_TOK:C_TOK + NC].unsqueeze(2).to_broadcast([P, NC, TILES]), ALU.mult))
                V.tensor_scalar(hot_p[k], hot_p[k], cst[:, C_P:C_P + 1], None, ALU.mult).then_inc(hots_ok, 1)

            dve.wait_ge(rowtile_ok, 1)
            for m in range(KS):
                shared_h(m, m)
                if m < TOPK:
                    hots(m)
            dve.wait_ge(map_mm, 1)
            V.tensor_copy(slot_tok[:, :], ps_map[:, 0:TILES]).then_inc(map_ok, 1)
            for t in range(TPG):
                add_x(0, t, 0, 16 * (t // 2 + 1))

            def expert_h(i, b, first):
                dve.wait_ge(eg_ok, i + 1)
                V.scalar_tensor_tensor(lge[:, b, :], ge[:, b, :], SLOPE, ge[:, b, :], ALU.mult, ALU.max).then_inc(elg_ok, 1)
                dve.wait_ge(elg_ok, i + 1)
                if not first:
                    dve.wait_ge(eh_tr, i - 1)
                V.tensor_tensor(he[:, b, :], lge[:, b, :], ps_gu[b][:, M:2 * M], ALU.mult).then_inc(eh_ok, 1)
                dve.wait_ge(eh_tr, i + 1)
                if not first:
                    dve.wait_ge(ey_mm, i - 1)
                V.tensor_copy(hts[:, b, :], ps_h[b][:, 0:M]).then_inc(eht_ok, 1)

            for i in range(U):
                expert_h(i, i % 2, i < 2)
            with dve.Fori(1, TILES // U) as j:
                for b in range(U):
                    expert_h(j * U + b, b % 2, False)

            def group(g, par, wait_store):
                for m in range(KS):
                    shared_h(g * KS + m, m)
                    combine(g - 1, m, 1 - par)
                for t in range(TPG):
                    if wait_store is not None:
                        dve.wait_ge(out_st[par * TPG + t], wait_store)
                    add_x(g, t, par, (g * (TPG // 2) + (t // 2 + 1)) * 16)

            group(1, 1, None)
            with dve.Fori(1, NG // 2) as j:
                group(j * 2, 0, j * 16)
                group(j * 2 + 1, 1, j * 16)
            for t in range(TPG):
                combine(NG - 1, t, 1)

        @block.tensor
        def _(pe):
            mm = nc.tensor.matmul
            ident = cst[:, C_ID:C_ID + P]
            pe.wait_ge(cst_in, 64)
            mm(ps_bias[0:NE, 0:NG], wg_sb[:, :], cond_sb[:, :], start=True, stop=True).then_inc(bias_mm, 1)

            def logits_tr(j):
                pe.wait_ge(lt_ok, j + 1)
                for t in range(TPG):
                    c = order[j] * TPG + t
                    last = nc.tensor.transpose(ps_log[:, c * NE:(c + 1) * NE], lt[:, j % 2, t * P:(t + 1) * P],
                                               ident[0:NE, 0:NE])
                last.then_inc(log_tr, 1)

            for j, g in enumerate(order):
                pe.wait_ge(xt_in[g % 2], 16 * (j // 2 + 1))
                if j >= 2:
                    pe.wait_ge(lt_ok, j - 1)
                for k in range(KH):
                    last = mm(ps_lt[j % 2][0:NE, :], wt_sb[:, k, :], xt[:, g % 2, k, :], start=k == 0, stop=k == KH - 1)
                last.then_inc(lt_mm, 1)
                if j >= 1:
                    logits_tr(j - 1)
            logits_tr(NG - 1)
            pe.wait_ge(cast, 1)
            pe.wait_ge(member_ok, 1)
            mem = member[:, :, :].rearrange("p c e -> p (c e)")
            mm(ps_rank[:, 0:NC * NE], tri[:, :], mem, start=True, stop=True)
            mm(ps_cnt[:, 0:NC * NE], ones[:, :], mem, start=True, stop=True).then_inc(rank_mm, 1)

            def gate_up(s, m, par, first):
                b = m % 2
                if not first:
                    pe.wait_ge(h_ok, s - 1)
                for w, ps in ((swg, ps_g), (swu, ps_u)):
                    for k in range(KH):
                        last = mm(ps[b][:, :], w[:, k, m * P:(m + 1) * P], xt[:, par, k, :], start=k == 0, stop=k == KH - 1)
                last.then_inc(gu_mm, 1)

            def down(g, t, first):
                c = g * TPG + t
                if not first:
                    pe.wait_ge(acc_ok, c - 1)
                for m in range(KS):
                    last = mm(ps_p[t % 2][:, :], ht[:, m, t * P:(t + 1) * P], swd[:, m, :], start=m == 0, stop=m == KS - 1)
                last.then_inc(p_mm, 1)

            pe.wait_ge(sw_in, 48)
            pe.wait_ge(rowtile_ok, 1)
            for m in range(KS):
                gate_up(m, m, 0, m < 2)
            pe.wait_ge(hots_ok, 2 * TOPK)
            n, total = 0, TOPK * NC * 2
            for k in range(TOPK):
                for c in range(NC):
                    for digit in (hot_p[k], hot_c[k]):
                        last = mm(ps_map[:, 0:TILES], hot_row[:, k, c, :], digit[:, c, :], start=n == 0, stop=n == total - 1)
                        n += 1
            last.then_inc(map_mm, 1)
            pe.wait_ge(h_ok, KS)
            for t in range(TPG):
                down(0, t, t < 2)

            def x_tr(i, b, b4, turn):
                pe.wait_ge(xg_in[b4], turn)
                for k in range(KH):
                    last = nc.tensor.transpose(ps_x[b][:, k * P:(k + 1) * P], xg[:, b4, k * P:(k + 1) * P], ident)
                last.then_inc(ex_tr, 1)

            def expert_gate_up(i, b, first, e):
                pe.wait_ge(ex_ok, i + 1)
                if not first:
                    pe.wait_ge(eh_ok, i - 1)
                w = wgu[:, :, :, :].rearrange("p e k n -> p (e k n)")
                for k in range(KH):
                    last = mm(ps_gu[b][:, :], xts[:, b, k * P:(k + 1) * P], w[:, bass.ds(e * (KH * 2 * M) + k * 2 * M, 2 * M)],
                              start=k == 0, stop=k == KH - 1)
                last.then_inc(eg_mm, 1)

            def h_tr(i, b):
                pe.wait_ge(eh_ok, i + 1)
                for m in range(KM):
                    last = nc.tensor.transpose(ps_h[b][:, m * P:(m + 1) * P], he[:, b, m * P:(m + 1) * P], ident)
                last.then_inc(eh_tr, 1)

            def expert_down(i, b, first, e):
                pe.wait_ge(eht_ok, i + 1)
                if not first:
                    pe.wait_ge(ey_ok, i - 1)
                w = wdn[:, :, :, :].rearrange("p e k n -> p (e k n)")
                for m in range(KM):
                    last = mm(ps_y[b][:, :], hts[:, b, m * P:(m + 1) * P], w[:, bass.ds(e * (KM * H) + m * H, H)],
                              start=m == 0, stop=m == KM - 1)
                last.then_inc(ey_mm, 1)

            def expert(i):
                return nc.tensor.value_load(tile_exp[0:1, bass.ds(i, 1)], min_val=0, max_val=NE - 1)

            pe.wait_ge(route_ok, 1)
            x_tr(0, 0, 0, 16)
            pe.wait_ge(ew_in, 16 * 3 * NE)
            pe.wait_ge(acc_ok, TPG)

            def turn(j, first=False, last=False):
                for b in range(U):
                    i = j * U + b
                    e = expert(i)
                    expert_gate_up(i, b % 2, first and b < 2, e)
                    if b < U - 1:
                        x_tr(i + 1, (b + 1) % 2, b + 1, j * 16 + 16)
                    elif not last:
                        x_tr(i + 1, 0, 0, j * 16 + 32)
                    if not (first and b == 0):
                        expert_down(i - 1, (b - 1) % 2, first and b < 3, expert(i - 1))
                    h_tr(i, b % 2)

            turn(0, first=True)
            with pe.Fori(1, TILES // U - 1) as j:
                turn(j)
            turn(TILES // U - 1, last=True)
            expert_down(TILES - 1, 1, False, expert(TILES - 1))

            pe.wait_ge(ey_ok, TILES)
            def group(g, par, loads):
                pe.wait_ge(xt_in[par], loads)
                for m in range(KS):
                    gate_up(g * KS + m, m, par, False)
                pe.wait_ge(h_ok, g * KS + KS)
                for t in range(TPG):
                    down(g, t, False)

            with pe.Fori(0, (NG - 2) // 2) as j:
                group(j * 2 + 1, 1, j * 16 + 16 * (NG // 2 + 1))
                group(j * 2 + 2, 0, j * 16 + 16 * (NG // 2 + 1))
            group(NG - 1, 1, 16 * (NG // 2 + NG // 2))


def kernel(**inputs):
    import numpy as np
    import concourse.bacc as bacc
    from concourse.bass_utils import run_bass_kernel_spmd

    def lay(a):
        return np.ascontiguousarray(a)

    pre = "L0_cond_"
    x = lay(inputs["x"]).reshape(T, H)
    p = np.arange(P)
    c = np.zeros((P, C_W), np.float32)
    c[:, C_ID:C_ID + P] = np.eye(P)
    c[:, C_TRI:C_TRI + P] = p[:, None] < p[None, :]
    c[:, C_IOTA:C_IOTA + P] = p[None, :]
    c[:, C_REV:C_REV + NE] = NE - np.arange(NE)
    c[:, C_SCAN:C_SCAN + NE * NC] = np.arange(NE * NC) % NC != 0
    c[:, C_P] = p
    c[:, C_TOK:C_TOK + NC] = P * np.arange(NC)
    arrays = {
        "x": x, "xT": lay(x.T), "wtT": lay(np.asarray(inputs[pre + "wt"]).T), "wgT": lay(np.asarray(inputs[pre + "wg"]).T),
        "condT": lay(np.asarray(inputs["cond_64"]).T),
        "w_gate": lay(inputs[pre + "w_gate"]), "w_up": lay(inputs[pre + "w_up"]), "w_down": lay(inputs[pre + "w_down"]),
        "sw_gate": lay(inputs[pre + "sw_gate"]), "sw_up": lay(inputs[pre + "sw_up"]), "sw_down": lay(inputs[pre + "sw_down"]),
        "consts": c,
    }
    nc = bacc.Bacc("TRN2", target_bir_lowering=False, num_devices=1)
    arrays = {f"in_{n}": a for n, a in arrays.items()}
    args = [nc.dram_tensor(n, a.shape, mybir.dt.from_np(a.dtype), kind="ExternalInput").ap() for n, a in arrays.items()]
    args.append(nc.dram_tensor("out_dram", (T, H), mybir.dt.float32, kind="ExternalOutput").ap())
    moe_kernel(nc, *args)
    r = run_bass_kernel_spmd(nc, [arrays], core_ids=[0])
    return r.results[0]["out_dram"].reshape(NG, GT, H)
```

```python
import concourse.bass as bass
from concourse import mybir
from contextlib import ExitStack

P = 128
T, H, NE, M, SM, G = 4096, 512, 8, 256, 512, 64
KH = H // P
KM = M // P
KS = SM // P
TOPK = 2
GT = 512
NG = T // GT
TPG = GT // P
NC = T // P
EARLY = 3
U = 4
TILES = -(-(T * TOPK // P + NE - 1) // U) * U
SLOPE = 0.01
SG, SU, SD, FIRST_E = 0, 1, 2, 3
CHUNKS = FIRST_E + 2 * NE
GU_PART = KH * 2 * M
DN_PART = KM * H
E_SIZE = 2 * (GU_PART + DN_PART)
STEP_CHUNKS = [[2], [3], [4], [5], [7], [], [8], [9], [12, 13], [14], [15], [16]]
DOWN_CHUNKS = [[6], [10, 11], [17, 18]]
LOADS = [[5, 6, 7, 8], [9, 10, 11, 12, 13], [14, 15, 16, 17, 18]]
STAGES = 3
HOTS_STEP = 5
C_ID, C_TRI, C_IOTA, C_REV, C_SCAN, C_TOK, C_W = 0, 128, 256, 384, 392, 648, 680


def moe_kernel(nc, x, xT, wtT, wgT, condT, w_gate, w_up, w_down, sw_gate, sw_up, sw_down, consts, out):
    F32, F32R, F16, BF16, I32 = (mybir.dt.float32, mybir.dt.float32r, mybir.dt.float16, mybir.dt.bfloat16,
                                 mybir.dt.int32)
    ALU, ACT, AX = mybir.AluOpType, mybir.ActivationFunctionType, mybir.AxisListType

    xT_v = xT.rearrange("(k p) t -> p k t", p=P)
    wtT_v = wtT.rearrange("(k p) e -> p k e", p=P)
    ctx = ExitStack()
    with ctx:
        def sb(name, shape, dt=F32):
            return ctx.enter_context(nc.sbuf_tensor(name, shape, dt))

        def under(name, shape, dt):
            with nc.sbuf_tensor(name, shape, dt) as t:
                return t

        def sem(name):
            return ctx.enter_context(nc.semaphore(name))

        def sems(name, n):
            return [sem(f"{name}{i}") for i in range(n)]

        WIDE = EARLY
        X_TURN = 1
        assert U == KH
        YW = 2 * TPG
        YB = 4
        slot_rows = nc.dram_tensor("slot_rows", (TILES * P, H), F32, kind="Internal").ap()

        ht_late = under("ht_late", [P, 2, KS, GT], F32R)
        wexp = sb("wexp", [P, NE * E_SIZE // 2])
        wexp16 = wexp[:, :].bitcast(F16)
        swgu = sb("swgu", [P, 2, 2, KH, SM], F16)
        swd = sb("swd", [P, 2, KS, H], F32R)

        def gu_part(e, part):
            at = e * E_SIZE + part * GU_PART
            return wexp16[:, at:at + GU_PART]

        def dn_part(e, part):
            at = e * E_SIZE + 2 * GU_PART + part * DN_PART
            return wexp16[:, at:at + DN_PART]

        cst = sb("cst", [P, C_W])
        tri = sb("tri", [P, P], BF16)
        ones = sb("ones", [P, P], BF16)
        wt_sb = sb("wt_sb", [P, KH, NE])
        wg_sb = sb("wg_sb", [G, NE])
        cond_sb = sb("cond_sb", [G, NG])
        bias_sb = sb("bias_sb", [NE, NG])
        pos = sb("pos", [P, TOPK, NC], I32)
        wts = sb("wts", [P, TOPK, NC])
        slot_tok = sb("slot_tok", [P, TILES], I32)
        tile_exp = sb("tile_exp", [1, TILES], I32)
        tile_f = sb("tile_f", [P, TILES])
        idx_e = sb("idx_e", [P, U], I32)
        idx_c = sb("idx_c", [P, YW, TOPK], I32)
        row_f = sb("row_f", [P, 2 * TOPK, NC])
        squares = sb("squares", [P, CHUNKS + 1])
        sq_all = sb("sq_all", [P, CHUNKS + 1])
        half_exp = sb("half_exp", [P, CHUNKS + 1], I32)
        scale = sb("scale", [P, CHUNKS + 1])
        inv = sb("inv", [P, CHUNKS + 1])
        x_squares = sb("x_squares", [P, NG])
        inv_sh = sb("inv_sh", [P, 2])
        inv_gu = sb("inv_gu", [P, TILES])
        inv_dn = sb("inv_dn", [P, TILES])
        h_sq = sb("h_sq", [P, U])
        h_exp = sb("h_exp", [P, U], I32)
        h_scale = sb("h_scale", [P, U])
        h_inv = sb("h_inv", [P, U])
        y_scale = sb("y_scale", [P, U])
        X = CHUNKS
        acc = sb("acc", [P, EARLY * TPG, H])
        xa = acc[:, (EARLY - 1) * TPG:EARLY * TPG, :]
        xb = sb("xb", [P, KH * GT])
        xhl_early = xb[:, :].bitcast(F16).rearrange("p (s k t) -> p s k t", s=2, k=KH)
        xts = xb[:, 0:1024].bitcast(F16).rearrange("p (b s c) -> p b s c", b=2, s=2)
        he = xb[:, 1024:1536].rearrange("p (b m) -> p b m", b=2)
        hts = xb[:, 1536:2048].bitcast(F16).rearrange("p (b s c) -> p b s c", b=2, s=2)
        gs_t = sb("gs_t", [P, 1024])
        gs = gs_t[:, :].rearrange("p (b t) -> p b t", b=2)
        ge = gs_t[:, 0:512].rearrange("p (b t) -> p b t", b=2)
        lt = gs_t[0:NE, :].rearrange("p (b t) -> p b t", b=2)
        ht_early = under("ht_early", [P, 2, KS, GT], F32R)
        htx = sb("htx", [P, 2 * KS * GT])
        xhl_late = htx[:, 0:2048].bitcast(F16).rearrange("p (s k t) -> p s k t", s=2, k=KH)
        xa_late = htx[:, 2048:4096].rearrange("p (k t) -> p k t", k=KH)
        area1 = sb("area1", [P, 2048])
        area2 = sb("area2", [P, 2048])
        xg = area1[:, :].rearrange("p (b h) -> p b h", b=U)
        z = area1[:, :].rearrange("p (b h) -> p b h", b=TPG)
        ysb = area2[:, :].rearrange("p (b h) -> p b h", b=U)
        yg = wexp[:, 4096:4096 + YB * TOPK * H].rearrange("p (b k h) -> p b k h", b=YB, k=TOPK)

        def flat(v):
            return v.rearrange("p c h -> p (c h)")

        def stage(n):
            if n < 2:
                return flat(acc[:, n * TPG:(n + 1) * TPG, :])
            return (area1[:, :], area2[:, :], hot_t[:, 3 * E_SIZE // 2 - 2048:3 * E_SIZE // 2])[(n - 2) % STAGES]

        def x_router(g):
            at = 5 * E_SIZE // 2 + (g - 4) * KH * GT
            return (flat(xa), xb[:, :], htx[:, 0:2048], htx[:, 2048:4096])[g] if g < 4 else wexp[:, at:at + KH * GT]

        def squared(n):
            return [q for q in ((n + 1, n + 2) if n == SD else (n + 2,)) if q < CHUNKS]

        def early(g):
            return isinstance(g, int) and g < EARLY

        scr = wexp[:, 4 * E_SIZE // 2:5 * E_SIZE // 2]
        hot_t = wexp[:, 5 * E_SIZE // 2:]
        hot_row = hot_t[:, 0:4096].bitcast(F16).rearrange("p (k c r) -> p k c r", k=TOPK, c=NC)
        hw = TILES * NC // 2
        hot_v = [hot_t[:, 4096 + k * hw:4096 + (k + 1) * hw].bitcast(F16).rearrange("p (c t) -> p c t", c=NC)
                 for k in range(TOPK)]
        dump = [scr[:, k * 1024:(k + 1) * 1024].bitcast(BF16) for k in range(2)]

        def s3(i):
            return scr[:, i * 256:(i + 1) * 256].rearrange("p (c e) -> p c e", e=NE)

        logit, prob, keep, eq = s3(0), s3(1), s3(2), s3(3)
        hot1, hot2, rank, tmp = s3(4), s3(5), s3(6), s3(7)
        cnt_ec = scr[:, 2048:2304].rearrange("p (e c) -> p e c", e=NE)
        cum_ec = scr[:, 2304:2560].rearrange("p (e c) -> p e c", e=NE)
        small = scr[:, 2560:2880].rearrange("p (n c) -> p n c", n=10)
        etmp = scr[:, 2880:2920].rearrange("p (n e) -> p n e", n=5)
        eint = scr[:, 2920:2928].bitcast(I32)
        row_i = scr[:, 2944:3072].bitcast(I32).rearrange("p (n c) -> p n c", n=2 * TOPK)
        member = sb("member", [P, NC, NE], BF16)
        tile_cmp = sb("tile_cmp", [P, TILES, NE])

        bank = [ctx.enter_context(nc.psum_tensor(f"bank{i}", [P, 512], F32)) for i in range(8)]
        ps_g, ps_u, ps_p = bank[0:2], bank[2:4], bank[4:8]
        ps_x, ps_gu, ps_h, ps_y = bank[0:2], bank[2:4], bank[4:6], bank[6:8]
        ps_lt, ps_bias, ps_log, ps_rank, ps_cnt, ps_map = bank[6:8], bank[4], bank[5], bank[4], bank[6], bank[1]

        wt_in, cst_in = sem("wt_in"), sem("cst_in")
        xt_in = sems("xt_in", NG)
        xa_in = sem("xa_in")
        ch_in = sems("ch_in", 4)
        x_in = sem("x_in")
        cast = sem("cast")
        bias_mm, bias_ok = sem("bias_mm"), sem("bias_ok")
        lt_mm, lt_ok, log_tr = sem("lt_mm"), sem("lt_ok"), sem("log_tr")
        r_step = sem("r_step")
        exp_in, exp_ok = sem("exp_in"), sem("exp_ok")
        member_ok, rank_mm, tokens_ok, route_ok = sem("member_ok"), sem("rank_mm"), sem("tokens_ok"), sem("route_ok")
        counts_ok, rows_ok, hots_ok, map_mm, map_ok = sem("counts_ok"), sem("rows_ok"), sem("hots_ok"), sem("map_mm"), sem("map_ok")
        xsq_act, xsq_dve, xsum_ok, xall_ok, xscale_ok = sem("xsq_act"), sem("xsq_dve"), sem("xsum_ok"), sem("xall_ok"), sem("xscale_ok")
        sq_ok, all_ok, scale_ok, hi_ok, lo_ok = sem("sq_ok"), sem("all_ok"), sem("scale_ok"), sem("hi_ok"), sem("lo_ok")
        xhi_ok, xlo_ok = sem("xhi_ok"), sem("xlo_ok")
        gu_mm, gs_ok, lg_ok, h_ok, hhi_ok, hlo_ok = (sem("gu_mm"), sem("gs_ok"), sem("lg_ok"), sem("h_ok"),
                                                     sem("hhi_ok"), sem("hlo_ok"))
        p_mm, p_ok = sem("p_mm"), sem("p_ok")
        eidx_ok, xg_in = sem("eidx_ok"), sems("xg_in", U)
        ex_tr, exhi_ok, exlo_ok, eg_mm, eg_ok, elg_ok, eh_ok = (sem("ex_tr"), sem("exhi_ok"), sem("exlo_ok"), sem("eg_mm"),
                                                                sem("eg_ok"), sem("elg_ok"), sem("eh_ok"))
        hsq_ok, hexp_ok, hscale_ok, hinv_ok, yscale_ok, hs_ok = (sem("hsq_ok"), sem("hexp_ok"), sem("hscale_ok"),
                                                                 sem("hinv_ok"), sem("yscale_ok"), sem("hs_ok"))
        eh_tr, ehhi_ok, ehlo_ok, ey_mm, ey_ok, y_out = (sem("eh_tr"), sem("ehhi_ok"), sem("ehlo_ok"), sem("ey_mm"),
                                                        sem("ey_ok"), sems("y_out", U))
        tiles_ok = sem("tiles_ok")
        cidx_ok, yg_in = sem("cidx_ok"), sems("yg_in", YB)
        half_ok, comb_ok = sem("half_ok"), sem("comb_ok")
        z_in, z_out, old_out = sems("z_in", TPG), sems("z_out", TPG), sem("old_out")

        block = ctx.enter_context(nc.Block())
        order = list(range(1, NG)) + [0]

        def chunk_loads(n):
            st = stage(n)
            v = st.rearrange("p (k n) -> p k n", k=KH)
            if n < FIRST_E:
                return [(v, (sw_gate, sw_up, sw_down)[n].rearrange("(k p) n -> p k n", p=P))]
            e = (n - FIRST_E) // 2
            if (n - FIRST_E) % 2:
                return [(st[:, 0:DN_PART].rearrange("p (k n) -> p k n", k=KM), w_down[e].rearrange("(k p) n -> p k n", p=P))]
            return [(v[:, :, 0:M], w_gate[e].rearrange("(k p) n -> p k n", p=P)),
                    (v[:, :, M:2 * M], w_up[e].rearrange("(k p) n -> p k n", p=P))]

        def chunk_arrived(n):
            return 16 * sum(len(chunk_loads(i)) for i in range(n % 4, n + 1, 4))

        def chunk_parts(n):
            st = stage(n)
            if n in (SG, SU):
                return st, swgu[:, n, 0].rearrange("p k n -> p (k n)"), swgu[:, n, 1].rearrange("p k n -> p (k n)")
            if n == SD:
                return st, swd[:, 0].rearrange("p k n -> p (k n)"), swd[:, 1].rearrange("p k n -> p (k n)")
            e = (n - FIRST_E) // 2
            if (n - FIRST_E) % 2:
                return st[:, 0:DN_PART], dn_part(e, 0), dn_part(e, 1)
            return st, gu_part(e, 0), gu_part(e, 1)

        @block.sync
        def _(sp):
            def load_chunk(n):
                if n == 1 + STAGES:
                    sp.wait_ge(lt_mm, NG)
                    sp.wait_ge(xsq_act, NG // 2)
                    sp.wait_ge(xsq_dve, NG // 2)
                if n >= 2 + STAGES:
                    sp.wait_ge(hi_ok, n - STAGES + 1)
                    sp.wait_ge(lo_ok, n - STAGES + 1)
                for dst, src in chunk_loads(n):
                    sp.dma_start(dst, src).then_inc(ch_in[n % 4], 16)

            sp.dma_start(wt_sb[:, :, :], wtT_v).then_inc(wt_in, 16)
            for j, g in enumerate(order):
                sp.dma_start(x_router(g).rearrange("p (k t) -> p k t", k=KH), xT_v[:, :, g * GT:(g + 1) * GT]
                             ).then_inc(xt_in[g], 16)
                if j == 0:
                    sp.dma_start(wg_sb[:, :], wgT).then_inc(cst_in, 16)
                    sp.dma_start(cond_sb[:, :], condT).then_inc(cst_in, 16)
                    sp.dma_start(cst[:, :], consts).then_inc(cst_in, 16)
                if j == 1:
                    load_chunk(SG)
                if j == 3:
                    load_chunk(SU)
            load_chunk(SD)
            load_chunk(FIRST_E)
            load_chunk(FIRST_E + 1)
            sp.wait_ge(lo_ok, 2)
            sp.wait_ge(hi_ok, 2)
            for g in range(EARLY):
                if g < EARLY - 1:
                    sp.dma_start(acc[:, g * TPG:(g + 1) * TPG, :],
                                 x[g * GT:(g + 1) * GT, :].rearrange("(c p) h -> p c h", p=P)).then_inc(x_in, 16)
                sp.wait_ge(xhi_ok, g * KH + KH)
                sp.wait_ge(xlo_ok, g * KH + KH)
                if g < EARLY - 1:
                    sp.dma_start(xa, xT_v[:, :, (g + 1) * GT:(g + 2) * GT]).then_inc(xa_in, 16)
                else:
                    sp.dma_start(xa, x[g * GT:(g + 1) * GT, :].rearrange("(c p) h -> p c h", p=P)).then_inc(x_in, 16)
                for n in LOADS[g]:
                    load_chunk(n)
            sp.wait_ge(p_mm, EARLY * TPG)
            sp.dma_start(xa_late, xT_v[:, :, EARLY * GT:(EARLY + 1) * GT]).then_inc(xa_in, 16)
            with sp.Fori(0, TILES // U) as j:
                for b in range(U):
                    sp.wait_ge(ey_ok, j * U + (b + 1))
                    sp.dma_start(slot_rows[bass.ds((j * U + b) * P, P), :], ysb[:, b, :]).then_inc(y_out[b], 16)

            def late(g, first=False, last=False, first_old=None, q0=None):
                for t in range(TPG):
                    if not first:
                        sp.wait_ge(z_out[t], g * 16 - 16 * EARLY)
                    sp.dma_start(z[:, t, :], x[bass.ds((g * TPG + t) * P, P), :]).then_inc(z_in[t], 16)
                if not last:
                    sp.wait_ge(xhi_ok, g * KH + KH)
                    sp.wait_ge(xlo_ok, g * KH + KH)
                    sp.dma_start(xa_late, xT_v[:, :, bass.ds(g * GT + GT, GT)]).then_inc(xa_in, 16)
                if first_old is not None:
                    for o in range(TPG):
                        sp.wait_ge(comb_ok, q0 + 2 * (o + 1))
                        sp.dma_start(out[bass.ds((first_old + o) * P, P), :], acc[:, bass.ds(first_old + o, 1), :]
                                     .rearrange("p o h -> p (o h)")).then_inc(old_out, 16)
                for t in range(TPG):
                    sp.wait_ge(p_ok, g * TPG + (t + 1))
                    sp.dma_start(out[bass.ds((g * TPG + t) * P, P), :], z[:, t, :]).then_inc(z_out[t], 16)

            sp.wait_ge(ex_tr, TILES)
            late(EARLY, first=True, first_old=0, q0=0)
            with sp.Fori(EARLY + 1, EARLY + WIDE) as g:
                late(g, first_old=g * TPG - TPG * EARLY, q0=g * YW - YW * EARLY)
            late(NG - 2)
            late(NG - 1, last=True)
            for t in range(TPG):
                sp.wait_ge(z_out[t], 16 * (NG - EARLY))
            sp.wait_ge(old_out, 16 * EARLY * TPG)

        @block.gpsimd
        def _(pool):
            def times_token(k):
                pool.wait_ge(hots_ok, k + 1)
                nc.gpsimd.tensor_tensor(hot_v[k], hot_v[k], cst[:, C_TOK:C_TOK + NC].unsqueeze(2)
                                        .to_broadcast([P, NC, TILES]), ALU.mult).then_inc(tokens_ok, 1)

            def all_sum(n):
                pool.wait_ge(sq_ok, n + 1)
                nc.gpsimd.partition_all_reduce(sq_all[:, n:n + 1], squares[:, n:n + 1], P, bass.bass_isa.ReduceOp.add).then_inc(all_ok, 1)

            for n in (SG, SU):
                all_sum(n)
            pool.wait_ge(xsum_ok, 1)
            nc.gpsimd.partition_all_reduce(sq_all[:, X:X + 1], squares[:, X:X + 1], P, bass.bass_isa.ReduceOp.add).then_inc(xall_ok, 1)
            def sums(n):
                for q in squared(n):
                    pool.wait_ge(sq_ok, q)
                    nc.gpsimd.partition_all_reduce(sq_all[:, q:q + 1], squares[:, q:q + 1], P,
                                                   bass.bass_isa.ReduceOp.add).then_inc(all_ok, 1)

            for g in range(EARLY):
                for m in range(KS):
                    s = g * KS + m
                    pool.wait_ge(hhi_ok, s + 1)
                    nc.gpsimd.tensor_tensor(ht_early[:, 1, m, :], gs[:, m % 2, :], ht_early[:, 0, m, :], ALU.subtract
                                            ).then_inc(hlo_ok, 1)
                    for n in STEP_CHUNKS[s]:
                        sums(n)
                    if s == HOTS_STEP:
                        times_token(0)
                    if s == HOTS_STEP + 1:
                        times_token(1)
                for n in DOWN_CHUNKS[g]:
                    sums(n)

            def index_x(i, b):
                nc.gpsimd.tensor_copy(idx_e[:, b:b + 1], slot_tok[:, bass.ds(i, 1)]).then_inc(eidx_ok, 1)

            def gather_x(b):
                nc.gpsimd.indirect_dma_start(out=xg[:, b, :], out_offset=None, in_=x,
                                             in_offset=bass.IndirectOffsetOnAxis(ap=idx_e[:, b:b + 1], axis=0)
                                             ).then_inc(xg_in[b], 16)

            def turn_x(j, b):
                i = j * U + b
                pool.wait_ge(ex_tr, i - (U - 2))
                pool.wait_ge(eidx_ok, i + 1)
                index_x(i + 1, (b + 1) % U)
                gather_x(b)

            pool.wait_ge(map_ok, 1)
            index_x(0, 0)
            pool.wait_ge(hi_ok, CHUNKS - 1)
            pool.wait_ge(lo_ok, CHUNKS - 1)
            for b in range(U - 1):
                pool.wait_ge(eidx_ok, b + 1)
                index_x(b + 1, b + 1)
                gather_x(b)
            turn_x(0, U - 1)
            with pool.Fori(1, TILES // U - 1) as j:
                for b in range(U):
                    turn_x(j, b)
            for b in range(U - 1):
                turn_x(TILES // U - 1, b)
            pool.wait_ge(ex_tr, TILES - U)
            pool.wait_ge(eidx_ok, TILES)
            gather_x(U - 1)

            def index_y(c, b):
                nc.gpsimd.tensor_copy(idx_c[:, b, :], pos[:, :, bass.ds(c, 1)].rearrange("p k o -> p (k o)")).then_inc(cidx_ok, 1)

            def gather_y(n, b):
                for k in range(TOPK):
                    nc.gpsimd.indirect_dma_start(out=yg[:, b, k, :], out_offset=None, in_=slot_rows,
                                                 in_offset=bass.IndirectOffsetOnAxis(ap=idx_c[:, n:n + 1, k:k + 1]
                                                                                     .rearrange("p n k -> p (n k)"), axis=0)
                                                 ).then_inc(yg_in[b], 16)

            def turn_y(q, n, c_next):
                if not isinstance(q, int) or q >= YB:
                    pool.wait_ge(comb_ok, q - (YB - 1))
                pool.wait_ge(cidx_ok, q + 1)
                index_y(c_next, (n + 1) % YW)
                gather_y(n, n % YB)

            def wide_order(g, old):
                return [c for t in range(TPG) for c in (g * TPG + t, old + t)] + [g * TPG + TPG]

            index_y(EARLY * TPG, 0)
            for b in range(U):
                pool.wait_ge(y_out[b], 16 * (TILES // U))
            tiles = wide_order(EARLY, 0)
            for n in range(YW):
                turn_y(n, n, tiles[n + 1])
            with pool.Fori(EARLY + 1, EARLY + WIDE) as g:
                tiles = wide_order(g, g * TPG - TPG * EARLY)
                for n in range(YW):
                    turn_y(g * YW + (n - YW * EARLY), n, tiles[n + 1])
            q0 = YW * WIDE
            for q in range(q0, NC - 1):
                turn_y(q, q % YW, (EARLY + WIDE) * TPG + q - q0 + 1)
            pool.wait_ge(comb_ok, NC - YB)
            pool.wait_ge(cidx_ok, NC)
            gather_y((NC - 1) % YW, (NC - 1) % YB)

        @block.scalar
        def _(act):
            A, C = nc.scalar.activation, ACT.Copy

            def square(n):
                act.wait_ge(ch_in[n % 4], chunk_arrived(n))
                v, high, _ = chunk_parts(n)
                A(high.bitcast(BF16), v, ACT.Square, accum_out=squares[:, n:n + 1]).then_inc(sq_ok, 1)

            def high(n):
                v, hi, _ = chunk_parts(n)
                if n == SD:
                    act.wait_ge(ch_in[n % 4], chunk_arrived(n))
                    A(hi, v, C).then_inc(hi_ok, 1)
                else:
                    act.wait_ge(scale_ok, n + 1 - (n > SD))
                    A(hi, v, C, scale=scale[:, n:n + 1]).then_inc(hi_ok, 1)

            def squares_behind(n):
                for q in squared(n):
                    if q == FIRST_E + 8:
                        act.wait_ge(route_ok, 1)
                    if q == FIRST_E + 10:
                        act.wait_ge(map_mm, 1)
                    if q == CHUNKS - 1:
                        act.wait_ge(lo_ok, CHUNKS - 2)
                    square(q)

            for j in range(1, NG, 2):
                act.wait_ge(xt_in[order[j]], 16)
                if j > 1:
                    act.wait_ge(xsq_act, j // 2)
                A(dump[0], x_router(order[j]), ACT.Square, accum_out=x_squares[:, j:j + 1]).then_inc(xsq_act, 1)
                if j == 1:
                    act.wait_ge(cst_in, 48)
                    A(tri[:, :], cst[:, C_TRI:C_TRI + P], C)
                    A(ones[:, :], cst[:, C_TRI:C_TRI + P], C, bias=1.0, scale=0.0).then_inc(cast, 1)
                    square(SG)
                if j == 3:
                    square(SU)
                    high(SG)
                if j == 5:
                    high(SU)

            def x_high(g):
                src, dst = (xa, xhl_early) if early(g) else (xa_late, xhl_late)
                if isinstance(g, int) and g == 0:
                    act.wait_ge(xscale_ok, 1)
                    act.wait_ge(lt_mm, order.index(1) + 1)
                else:
                    act.wait_ge(xa_in, g * 16)
                    act.wait_ge(gu_mm, g * KS)
                for k in range(KH):
                    A(dst[:, 0, k, :], src[:, k, :], C, scale=scale[:, X:X + 1]).then_inc(xhi_ok, 1)

            def shared_gate(s, b, first=False):
                act.wait_ge(gu_mm, s + 1)
                if not first:
                    act.wait_ge(hlo_ok, s - 1)
                A(gs[:, b, :], ps_g[b][:, :], C, scale=inv_sh[:, 0:1]).then_inc(gs_ok, 1)

            def h_high(s, m, ht):
                act.wait_ge(h_ok, s + 1)
                A(ht[:, 0, m, :], gs[:, m % 2, :], C).then_inc(hhi_ok, 1)

            x_high(0)
            act.wait_ge(exp_in, 1)
            A(prob, keep, ACT.Exp).then_inc(exp_ok, 1)
            for g in range(EARLY):
                for m in range(KS):
                    s = g * KS + m
                    shared_gate(s, m % 2, first=s < 2)
                    for n in STEP_CHUNKS[s]:
                        high(n)
                    h_high(s, m, ht_early)
                    if m == KS - 1 and g + 1 < EARLY:
                        x_high(g + 1)
                    for n in STEP_CHUNKS[s]:
                        squares_behind(n)
                for n in DOWN_CHUNKS[g]:
                    high(n)
                    squares_behind(n)

            def x_high_e(i, b):
                act.wait_ge(ex_tr, i + 1)
                A(xts[:, b, 0, :], ps_x[b][:, :], C, scale=scale[:, X:X + 1]).then_inc(exhi_ok, 1)

            def gate_out(i, b, first=False):
                act.wait_ge(eg_mm, i + 1)
                if not first:
                    act.wait_ge(hsq_ok, i - 1)
                A(ge[:, b, :], ps_gu[b][:, 0:M], C, scale=inv_gu[:, bass.ds(i, 1)]).then_inc(eg_ok, 1)

            def h_square(i, b, b4):
                act.wait_ge(eh_ok, i + 1)
                A(ge[:, b, :], he[:, b, :], ACT.Square, accum_out=h_sq[:, b4:b4 + 1]).then_inc(hsq_ok, 1)

            def h_high_e(i, b):
                act.wait_ge(eh_tr, i + 1)
                A(hts[:, b, 0, :], ps_h[b][:, 0:M], C).then_inc(ehhi_ok, 1)

            def y_rows(i, b, b4, stored):
                act.wait_ge(ey_mm, i + 1)
                if stored is not None:
                    act.wait_ge(y_out[b4], stored)
                A(ysb[:, b4, :], ps_y[b][:, :], C, scale=y_scale[:, b4:b4 + 1]).then_inc(ey_ok, 1)

            def turn(j, last=False):
                static = isinstance(j, int)
                for b in range(U):
                    i = j * U + b
                    gate_out(i, b % 2, first=static and i < 2)
                    if not (last and b >= U - 2):
                        x_high_e(i + 2, b % 2)
                    if not (static and i < 1):
                        h_high_e(i - 1, (b - 1) % 2)
                    h_square(i, b % 2, b)
                    if b >= 2:
                        y_rows(i - 2, b % 2, b - 2, None if static and j == 0 else j * 16)
                    elif not (static and j == 0):
                        y_rows(i - 2, b % 2, b + 2, None if static and j == 1 else j * 16 - 16)
                    if static and j == X_TURN:
                        if b == 0:
                            act.wait_ge(xa_in, EARLY * 16)
                        A(xhl_late[:, 0, b, :], xa_late[:, b, :], C, scale=scale[:, X:X + 1]).then_inc(xhi_ok, 1)

            x_high_e(0, 0)
            x_high_e(1, 1)
            act.wait_ge(tiles_ok, 1)
            turn(0)
            turn(1)
            with act.Fori(2, TILES // U - 1) as j:
                turn(j)
            turn(TILES // U - 1, last=True)
            h_high_e(TILES - 1, 1)
            for i in (TILES - 2, TILES - 1):
                y_rows(i, i % 2, i % U, 16 * (TILES // U - 1))

            act.wait_ge(hsq_ok, TILES)
            act.wait_ge(eh_ok, TILES)
            for m in range(KS):
                shared_gate(EARLY * KS + m, m % 2)
                h_high(EARLY * KS + m, m, ht_late)
            with act.Fori(EARLY + 1, NG) as g:
                x_high(g)
                for m in range(KS):
                    shared_gate(g * KS + m, m % 2)
                    h_high(g * KS + m, m, ht_late)

        @block.vector
        def _(dve):
            step = [0]

            def then(ins):
                step[0] += 1
                ins.then_inc(r_step, 1)
                dve.wait_ge(r_step, step[0])

            def bc(v):
                return v.unsqueeze(2).to_broadcast([P, NC, NE])

            V = nc.vector
            TWO23 = float(1 << 23)

            def power(sq, ex, sc, iv):
                then(V.tensor_scalar(ex, sq.bitcast(I32), 24, None, ALU.logical_shift_right))
                V.tensor_scalar(sc.bitcast(I32), ex, -TWO23, 204 * TWO23, ALU.mult, ALU.add)
                return V.tensor_scalar(iv.bitcast(I32), ex, TWO23, 50 * TWO23, ALU.mult, ALU.add)

            def chunk_scale(n):
                dve.wait_ge(all_ok, n + 1 - (n > SD))
                c = slice(n, n + 1)
                power(sq_all[:, c], half_exp[:, c], scale[:, c], inv[:, c]).then_inc(scale_ok, 1)

            def chunk_low(n):
                v, hi, lo = chunk_parts(n)
                dve.wait_ge(hi_ok, n + 1)
                if n == SD:
                    V.tensor_tensor(lo, v, hi, ALU.subtract).then_inc(lo_ok, 1)
                else:
                    V.scalar_tensor_tensor(lo, v, scale[:, n:n + 1], hi, ALU.mult, ALU.subtract).then_inc(lo_ok, 1)

            def x_scale():
                dve.wait_ge(xsq_act, NG // 2)
                dve.wait_ge(xsq_dve, NG // 2)
                V.tensor_reduce(squares[:, X:X + 1], x_squares[:, :], AX.X, ALU.add).then_inc(xsum_ok, 1)
                dve.wait_ge(xall_ok, 1)
                then(power(sq_all[:, X:X + 1], half_exp[:, X:X + 1], scale[:, X:X + 1], inv[:, X:X + 1]))
                V.tensor_scalar(inv_sh[:, :], inv[:, SG:SU + 1], inv[:, X:X + 1], None, ALU.mult).then_inc(xscale_ok, 1)

            for j, g in enumerate(order):
                if j % 2 == 0:
                    dve.wait_ge(xt_in[g], 16)
                    if j:
                        dve.wait_ge(xsq_dve, j // 2)
                    V.scalar_tensor_tensor(dump[1], x_router(g), 1.0, x_router(g), ALU.mult, ALU.mult,
                                           accum_out=x_squares[:, j:j + 1]).then_inc(xsq_dve, 1)
                if j == 0:
                    dve.wait_ge(bias_mm, 1)
                    V.tensor_copy(bias_sb[:, :], ps_bias[0:NE, 0:NG]).then_inc(bias_ok, 1)
                    dve.wait_ge(bias_ok, 1)
                if j == NG - 1:
                    x_scale()
                dve.wait_ge(lt_mm, j + 1)
                if j >= 2:
                    dve.wait_ge(log_tr, j - 1)
                V.tensor_scalar(lt[:, j % 2, :], ps_lt[j % 2][0:NE, :], bias_sb[:, g:g + 1], 0.5,
                                ALU.add, ALU.mult).then_inc(lt_ok, 1)
                if j == 1:
                    chunk_scale(SG)
                if j == 3:
                    chunk_scale(SU)
                    chunk_low(SG)
                if j == 5:
                    chunk_low(SU)
            def x_low(g):
                src, dst = (xa, xhl_early) if early(g) else (xa_late, xhl_late)
                for k in range(KH):
                    dve.wait_ge(xhi_ok, g * KH + (k + 1))
                    V.scalar_tensor_tensor(dst[:, 1, k, :], src[:, k, :], scale[:, X:X + 1], dst[:, 0, k, :],
                                           ALU.mult, ALU.subtract).then_inc(xlo_ok, 1)

            mx, den, m1, m2, r1, r2, wsum = (small[:, i] for i in range(7))
            dve.wait_ge(log_tr, NG)
            then(V.tensor_copy(logit, ps_log[:, 0:NC * NE].rearrange("p (c e) -> p c e", e=NE)))
            then(V.tensor_reduce(mx, logit, AX.X, ALU.max))
            V.tensor_tensor(keep, logit, bc(mx), ALU.subtract).then_inc(exp_in, 1)
            x_low(0)
            dve.wait_ge(exp_ok, 1)
            then(V.tensor_reduce(den, prob, AX.X, ALU.add))
            then(V.reciprocal(den, den))
            then(V.tensor_tensor(prob, prob, bc(den), ALU.mult))
            rev = cst[:, C_REV:C_REV + NE].unsqueeze(1).to_broadcast([P, NC, NE])
            then(V.tensor_reduce(m1, prob, AX.X, ALU.max))
            then(V.tensor_tensor(eq, prob, bc(m1), ALU.is_equal))
            then(V.tensor_tensor(eq, eq, rev, ALU.mult))
            then(V.tensor_reduce(r1, eq, AX.X, ALU.max))
            then(V.tensor_tensor(hot1, rev, bc(r1), ALU.is_equal))
            then(V.scalar_tensor_tensor(keep, hot1, -2.0, prob, ALU.mult, ALU.add))
            then(V.tensor_reduce(m2, keep, AX.X, ALU.max))
            then(V.tensor_tensor(eq, keep, bc(m2), ALU.is_equal))
            then(V.tensor_tensor(eq, eq, rev, ALU.mult))
            then(V.tensor_reduce(r2, eq, AX.X, ALU.max))
            then(V.tensor_tensor(hot2, rev, bc(r2), ALU.is_equal))
            V.tensor_tensor(member[:, :, :], hot1, hot2, ALU.add).then_inc(member_ok, 1)

            end = etmp[:, 2]

            def weights():
                then(V.tensor_tensor(wsum, m1, m2, ALU.add))
                then(V.tensor_scalar(wsum, wsum, 1e-20, None, ALU.add))
                then(V.reciprocal(wsum, wsum))
                V.tensor_tensor(wts[:, 0, :], m1, wsum, ALU.mult)
                V.tensor_tensor(wts[:, 1, :], m2, wsum, ALU.mult)

            def positions():
                dve.wait_ge(rank_mm, 1)
                V.tensor_copy(rank, ps_rank[:, 0:NC * NE].rearrange("p (c e) -> p c e", e=NE))
                V.tensor_copy(cnt_ec, ps_cnt[:, 0:NC * NE].rearrange("p (c e) -> p e c", e=NE)).then_inc(counts_ok, 1)
                dve.wait_ge(counts_ok, 1)
                cnt_f = cnt_ec.rearrange("p e c -> p (e c)")
                cum_f = cum_ec.rearrange("p e c -> p (e c)")
                then(V.tensor_tensor_scan(cum_f, cst[:, C_SCAN:C_SCAN + NE * NC], cnt_f, 0.0, ALU.mult, ALU.add))
                then(V.tensor_tensor(cnt_ec, cum_ec, cnt_ec, ALU.subtract))
                then(V.tensor_tensor(rank, rank, cnt_ec.rearrange("p e c -> p c e"), ALU.add))

            def tiles_of_experts():
                tot, tiles, _, base, one = (etmp[:, i] for i in range(5))
                then(V.tensor_scalar(tot, cum_ec[:, :, NC - 1], float(P - 1), None, ALU.add))
                then(V.tensor_copy(eint, tot))
                then(V.tensor_scalar(eint, eint, 7, None, ALU.logical_shift_right))
                then(V.tensor_copy(tiles, eint))
                then(V.memset(one, 1.0))
                then(V.tensor_tensor_scan(end, one, tiles, 0.0, ALU.mult, ALU.add))
                then(V.tensor_tensor(base, end, tiles, ALU.subtract))
                then(V.tensor_scalar(base, base, float(P), None, ALU.mult))
                then(V.tensor_tensor(rank, rank, base.unsqueeze(1).to_broadcast([P, NC, NE]), ALU.add))

            def slots():
                for k, hot in enumerate((hot1, hot2)):
                    then(V.tensor_tensor(tmp, hot, rank, ALU.mult))
                    then(V.tensor_reduce(small[:, 8 + k], tmp, AX.X, ALU.add))
                then(V.tensor_copy(pos[:, :, :], small[:, 8:10, :]))
                V.tensor_scalar(row_i[:, 0:TOPK, :], pos[:, :, :], P - 1, None, ALU.bitwise_and)
                then(V.tensor_scalar(row_i[:, TOPK:2 * TOPK, :], pos[:, :, :], 7, None, ALU.logical_shift_right))
                then(V.tensor_copy(row_f[:, :, :], row_i[:, :, :]))
                tb = [P, TILES, NE]
                then(V.tensor_tensor(tile_cmp[:, :, :], end.unsqueeze(1).to_broadcast(tb),
                                     cst[:, C_IOTA:C_IOTA + TILES].unsqueeze(2).to_broadcast(tb), ALU.is_le))
                then(V.tensor_reduce(tile_f[:, :], tile_cmp[:, :, :], AX.X, ALU.add))
                then(V.tensor_scalar(tile_f[:, :], tile_f[:, :], float(NE - 1), None, ALU.min))
                V.tensor_copy(tile_exp[:, :], tile_f[0:1, :]).then_inc(route_ok, 1)

            def tile_hots():
                tb = [P, TILES, NE]
                then(V.tensor_tensor(tile_cmp[:, :, :], cst[:, C_IOTA:C_IOTA + NE].unsqueeze(1).to_broadcast(tb),
                                     tile_f[:, :].unsqueeze(2).to_broadcast(tb), ALU.is_equal))

            def tile_scales():
                tb = [P, TILES, NE]
                prod = gs_t[:, 0:TILES * NE].rearrange("p (t e) -> p t e", e=NE)
                dve.wait_ge(hlo_ok, EARLY * KS)
                igu = inv[:, FIRST_E:CHUNKS:2]
                idn = inv[:, FIRST_E + 1:CHUNKS:2]
                for src, dst in ((igu, inv_gu), (idn, inv_dn)):
                    then(V.tensor_tensor(prod, tile_cmp[:, :, :], src.unsqueeze(1).to_broadcast(tb), ALU.mult))
                    then(V.tensor_reduce(dst[:, :], prod, AX.X, ALU.add))
                V.tensor_scalar(inv_gu[:, :], inv_gu[:, :], inv[:, X:X + 1], None, ALU.mult).then_inc(tiles_ok, 1)
                dve.wait_ge(tiles_ok, 1)

            def hot_tiles(k):
                V.tensor_tensor(hot_v[k], cst[:, C_IOTA:C_IOTA + TILES].unsqueeze(1).to_broadcast([P, NC, TILES]),
                                row_f[:, TOPK + k].unsqueeze(2).to_broadcast([P, NC, TILES]), ALU.is_equal
                                ).then_inc(hots_ok, 1)

            def hot_rows(k):
                V.tensor_tensor(hot_row[:, k], cst[:, C_IOTA:C_IOTA + P].unsqueeze(1).to_broadcast([P, NC, P]),
                                row_f[:, k].unsqueeze(2).to_broadcast([P, NC, P]), ALU.is_equal).then_inc(rows_ok, 1)

            def shared_h(s, m, ht, chunks=()):
                b = m % 2
                g = gs[:, b, :]
                dve.wait_ge(gs_ok, s + 1)
                V.scalar_tensor_tensor(g, g, SLOPE, g, ALU.mult, ALU.max).then_inc(lg_ok, 1)
                dve.wait_ge(lg_ok, s + 1)
                V.scalar_tensor_tensor(g, ps_u[b][:, :], inv_sh[:, 1:2], g, ALU.mult, ALU.mult).then_inc(h_ok, 1)
                for n in chunks:
                    chunk_low(n)
                if ht is ht_late:
                    dve.wait_ge(hhi_ok, s + 1)
                    V.tensor_tensor(ht[:, 1, m, :], g, ht[:, 0, m, :], ALU.subtract).then_inc(hlo_ok, 1)

            def add_p(rows, g, t):
                dve.wait_ge(p_mm, g * TPG + (t + 1))
                V.tensor_tensor(rows, ps_p[t][:, :], rows, ALU.add).then_inc(p_ok, 1)

            def scales(chunks):
                for n in chunks:
                    if n != SD:
                        chunk_scale(n)

            routing = {1: [weights], 2: [positions], HOTS_STEP: [lambda: hot_tiles(0), lambda: hot_tiles(1)],
                       6: [lambda: hot_rows(0)], 7: [lambda: hot_rows(1)], 2 * KS: [tile_hots]}
            for g in range(EARLY):
                for m in range(KS):
                    s = g * KS + m
                    if s == 2 * KS:
                        dve.wait_ge(map_mm, 1)
                        V.tensor_scalar(slot_tok[:, :], ps_map[:, 0:TILES], float(T // 2), None, ALU.add).then_inc(map_ok, 1)
                    scales(STEP_CHUNKS[s])
                    shared_h(s, m, ht_early, STEP_CHUNKS[s])
                    for part in routing.get(s, ()):
                        part()
                if g + 1 < EARLY:
                    x_low(g + 1)
                if g == 0:
                    tiles_of_experts()
                    slots()
                dve.wait_ge(x_in, 16 * (g + 1))
                chunks = DOWN_CHUNKS[g]
                scales(chunks[:1])
                for i, n in enumerate(chunks):
                    scales(chunks[i + 1:i + 2])
                    if n == CHUNKS - 1:
                        tile_scales()
                    chunk_low(n)
                if g < EARLY - 1:
                    for t in range(TPG):
                        add_p(acc[:, g * TPG + t, :], g, t)

            def expert_h(i, b, b4, first, last=False):
                g, h = ge[:, b, :], he[:, b, :]
                dve.wait_ge(eg_ok, i + 1)
                V.scalar_tensor_tensor(g, g, SLOPE, g, ALU.mult, ALU.max).then_inc(elg_ok, 1)
                dve.wait_ge(elg_ok, i + 1)
                if not first:
                    dve.wait_ge(eh_tr, i - 1)
                V.scalar_tensor_tensor(h, ps_gu[b][:, M:2 * M], inv_gu[:, bass.ds(i, 1)], g, ALU.mult, ALU.mult
                                       ).then_inc(eh_ok, 1)
                if not last:
                    x_low_e(i + 2, b)
                c = slice(b4, b4 + 1)
                dve.wait_ge(hsq_ok, i + 1)
                V.tensor_scalar(h_exp[:, c], h_sq[:, c].bitcast(I32), 24, None, ALU.logical_shift_right).then_inc(hexp_ok, 1)
                dve.wait_ge(hexp_ok, i + 1)
                V.tensor_scalar(h_scale[:, c].bitcast(I32), h_exp[:, c], -TWO23, 204 * TWO23, ALU.mult, ALU.add
                                ).then_inc(hscale_ok, 1)
                V.tensor_scalar(h_inv[:, c].bitcast(I32), h_exp[:, c], TWO23, 50 * TWO23, ALU.mult, ALU.add
                                ).then_inc(hinv_ok, 1)
                dve.wait_ge(hscale_ok, i + 1)
                V.tensor_scalar(h, h, h_scale[:, c], None, ALU.mult).then_inc(hs_ok, 1)
                dve.wait_ge(hinv_ok, i + 1)
                V.tensor_tensor(y_scale[:, c], h_inv[:, c], inv_dn[:, bass.ds(i, 1)], ALU.mult).then_inc(yscale_ok, 1)

            def x_low_e(i, b):
                dve.wait_ge(exhi_ok, i + 1)
                V.scalar_tensor_tensor(xts[:, b, 1, :], ps_x[b][:, :], scale[:, X:X + 1], xts[:, b, 0, :],
                                       ALU.mult, ALU.subtract).then_inc(exlo_ok, 1)

            def h_low_e(i, b):
                dve.wait_ge(ehhi_ok, i + 1)
                V.tensor_tensor(hts[:, b, 1, :], ps_h[b][:, 0:M], hts[:, b, 0, :], ALU.subtract).then_inc(ehlo_ok, 1)

            x_low_e(0, 0)
            x_low_e(1, 1)
            for t in range(TPG):
                add_p(acc[:, (EARLY - 1) * TPG + t, :], EARLY - 1, t)
            for i in range(U * (X_TURN + 1)):
                b = i % U
                if i >= U:
                    dve.wait_ge(ey_ok, i - 3)
                expert_h(i, b % 2, b, i < 2)
                if i >= 1:
                    h_low_e(i - 1, (b - 1) % 2)
                if i >= U * X_TURN:
                    dve.wait_ge(xhi_ok, EARLY * KH + b + 1)
                    V.scalar_tensor_tensor(xhl_late[:, 1, b, :], xa_late[:, b, :], scale[:, X:X + 1], xhl_late[:, 0, b, :],
                                           ALU.mult, ALU.subtract).then_inc(xlo_ok, 1)
            with dve.Fori(X_TURN + 1, TILES // U - 1) as j:
                for b in range(U):
                    dve.wait_ge(ey_ok, j * U + (b - 3))
                    expert_h(j * U + b, b % 2, b, False)
                    h_low_e(j * U + (b - 1), (b - 1) % 2)
            for b in range(U):
                i = TILES - U + b
                dve.wait_ge(ey_ok, i - 3)
                expert_h(i, b % 2, b, False, last=b >= U - 2)
                h_low_e(i - 1, (b - 1) % 2)
            h_low_e(TILES - 1, 1)

            def combine(rows, c, q, b, turns):
                dve.wait_ge(yg_in[b], turns * 32)
                V.scalar_tensor_tensor(rows, yg[:, b, 0, :], wts[:, 0, bass.ds(c, 1)], rows, ALU.mult, ALU.add
                                       ).then_inc(half_ok, 1)
                dve.wait_ge(half_ok, q + 1)
                return V.scalar_tensor_tensor(rows, yg[:, b, 1, :], wts[:, 1, bass.ds(c, 1)], rows, ALU.mult, ALU.add
                                              ).then_inc(comb_ok, 1)

            def late(g, q0, first_old=None):
                per = 2 if first_old is not None else 1
                n = 0
                for m in range(KS):
                    shared_h(g * KS + m, m, ht_late)
                    if m == KS - 1 and not (isinstance(g, int) and g == NG - 1):
                        x_low(g + 1)
                    for _ in range((0, per, per, 2 * per)[m]):
                        t = n // per
                        q = q0 + n
                        turns = q // YB + 1 if isinstance(q, int) else g * (YW // YB) + (n // YB + 1 - EARLY * YW // YB)
                        if n % per == 0:
                            dve.wait_ge(z_in[t], g * 16 - 16 * (EARLY - 1))
                            combine(z[:, t, :], g * TPG + t, q, n % YB, turns)
                        else:
                            row = acc[:, bass.ds(first_old + t, 1), :].rearrange("p o h -> p (o h)")
                            combine(row, first_old + t, q, n % YB, turns)
                        n += 1
                for t in range(TPG):
                    dve.wait_ge(comb_ok, q0 + n)
                    add_p(z[:, t, :], g, t)

            late(EARLY, 0, first_old=0)
            with dve.Fori(EARLY + 1, EARLY + WIDE) as g:
                late(g, g * YW - YW * EARLY, first_old=g * TPG - TPG * EARLY)
            late(NG - 2, YW * WIDE)
            late(NG - 1, YW * WIDE + TPG)

        @block.tensor
        def _(pe):
            mm = nc.tensor.matmul
            ident = cst[:, C_ID:C_ID + P]
            PASSES = ((0, 0), (0, 1), (1, 0))
            pe.wait_ge(wt_in, 16)

            def logits_tr(j):
                pe.wait_ge(lt_ok, j + 1)
                for t in range(TPG):
                    c = order[j] * TPG + t
                    last = nc.tensor.transpose(ps_log[:, c * NE:(c + 1) * NE], lt[:, j % 2, t * P:(t + 1) * P],
                                               ident[0:NE, 0:NE])
                last.then_inc(log_tr, 1)

            for j, g in enumerate(order):
                pe.wait_ge(xt_in[g], 16)
                if j >= 2:
                    pe.wait_ge(lt_ok, j - 1)
                for k in range(KH):
                    last = mm(ps_lt[j % 2][0:NE, :], wt_sb[:, k, :], x_router(g)[:, k * GT:(k + 1) * GT],
                              start=k == 0, stop=k == KH - 1)
                last.then_inc(lt_mm, 1)
                if j == 0:
                    pe.wait_ge(cst_in, 48)
                    mm(ps_bias[0:NE, 0:NG], wg_sb[:, :], cond_sb[:, :], start=True, stop=True).then_inc(bias_mm, 1)
                if j >= 1:
                    logits_tr(j - 1)
            logits_tr(NG - 1)

            def gate_up(s, m, g, first=False):
                b = m % 2
                xhl = xhl_early if early(g) else xhl_late
                if not first:
                    pe.wait_ge(h_ok, s - 1)
                for which, ps in ((0, ps_g), (1, ps_u)):
                    n = 0
                    for k in range(KH):
                        if m == 0 and which == 0:
                            pe.wait_ge(xlo_ok, g * KH + (k + 1))
                        for wp, xp in PASSES:
                            last = mm(ps[b][:, :], swgu[:, which, wp, k, m * P:(m + 1) * P], xhl[:, xp, k, :],
                                      start=n == 0, stop=n == 3 * KH - 1)
                            n += 1
                last.then_inc(gu_mm, 1)

            def down(g, blocks):
                ht = ht_early if early(g) else ht_late
                for t in range(TPG):
                    if blocks[0] == 0 and not (early(g) and g == 0):
                        pe.wait_ge(p_ok, g * TPG + (t + 1 - TPG))
                    for m in blocks:
                        for n, (hp, wp) in enumerate(PASSES):
                            last = mm(ps_p[t][:, :], ht[:, hp, m, t * P:(t + 1) * P], swd[:, wp, m, :],
                                      start=m == 0 and n == 0, stop=m == KS - 1 and n == 2)
                    if blocks[-1] == KS - 1:
                        last.then_inc(p_mm, 1)

            def downs(g, between=None):
                pe.wait_ge(hlo_ok, g * KS + KS - 1)
                down(g, range(KS - 1))
                if between is not None:
                    between()
                pe.wait_ge(hlo_ok, g * KS + KS)
                down(g, [KS - 1])

            def slot_map():
                pe.wait_ge(rows_ok, TOPK)
                pe.wait_ge(tokens_ok, TOPK)
                pe.wait_ge(h_ok, 2 * KS)
                n = 0
                for k in range(TOPK):
                    for c in range(NC):
                        last = mm(ps_map[:, 0:TILES], hot_row[:, k, c, :], hot_v[k][:, c, :],
                                  start=n == 0, stop=n == TOPK * NC - 1)
                        n += 1
                last.then_inc(map_mm, 1)

            pe.wait_ge(lo_ok, 2)
            for g in range(EARLY):
                for m in range(KS):
                    s = g * KS + m
                    if s == 2 * KS + 1:
                        pe.wait_ge(map_ok, 1)
                    gate_up(s, m, g, first=s < 2)
                    if s == 1:
                        pe.wait_ge(cast, 1)
                        pe.wait_ge(member_ok, 1)
                        mem = member[:, :, :].rearrange("p c e -> p (c e)")
                        mm(ps_rank[:, 0:NC * NE], tri[:, :], mem, start=True, stop=True)
                        mm(ps_cnt[:, 0:NC * NE], ones[:, :], mem, start=True, stop=True).then_inc(rank_mm, 1)
                if g == 0:
                    pe.wait_ge(counts_ok, 1)
                    pe.wait_ge(lo_ok, SD + 1)
                downs(g, between=slot_map if g == 1 else None)

            def x_tr(i, b, b4, turn):
                pe.wait_ge(xg_in[b4], turn)
                for k in range(KH):
                    last = nc.tensor.transpose(ps_x[b][:, k * P:(k + 1) * P], xg[:, b4, k * P:(k + 1) * P], ident)
                last.then_inc(ex_tr, 1)

            def expert_gate_up(i, b, first, e):
                pe.wait_ge(exlo_ok, i + 1)
                if not first:
                    pe.wait_ge(eh_ok, i - 1)
                n = 0
                for wp in range(2):
                    for k in range(KH):
                        w = wexp16[:, bass.ds(e * E_SIZE + (wp * GU_PART + k * 2 * M), 2 * M)]
                        for xp in range(2 - wp):
                            last = mm(ps_gu[b][:, :], xts[:, b, xp, k * P:(k + 1) * P], w, start=n == 0, stop=n == 3 * KH - 1)
                            n += 1
                last.then_inc(eg_mm, 1)

            def h_tr(i, b):
                pe.wait_ge(hs_ok, i + 1)
                for m in range(KM):
                    last = nc.tensor.transpose(ps_h[b][:, m * P:(m + 1) * P], he[:, b, m * P:(m + 1) * P], ident)
                last.then_inc(eh_tr, 1)

            def expert_down(i, b, first, e):
                pe.wait_ge(ehlo_ok, i + 1)
                pe.wait_ge(yscale_ok, i + 1)
                if not first:
                    pe.wait_ge(ey_ok, i - 1)
                n = 0
                for wp in range(2):
                    for m in range(KM):
                        w = wexp16[:, bass.ds(e * E_SIZE + (2 * GU_PART + wp * DN_PART + m * H), H)]
                        for hp in range(2 - wp):
                            last = mm(ps_y[b][:, :], hts[:, b, hp, m * P:(m + 1) * P], w, start=n == 0, stop=n == 3 * KM - 1)
                            n += 1
                last.then_inc(ey_mm, 1)

            def expert(i):
                return nc.tensor.value_load(tile_exp[0:1, bass.ds(i, 1)], min_val=0, max_val=NE - 1)

            pe.wait_ge(route_ok, 1)
            x_tr(0, 0, 0, 16)
            x_tr(1, 1, 1, 16)

            def turn(j, last=False):
                static = isinstance(j, int)
                for b in range(U):
                    i = j * U + b
                    expert_gate_up(i, b % 2, static and i < 2, expert(i))
                    if b < U - 2:
                        x_tr(i + 2, b % 2, b + 2, j * 16 + 16)
                    elif not last:
                        x_tr(i + 2, b % 2, b + 2 - U, j * 16 + 32)
                    if static and i == 1:
                        pe.wait_ge(p_ok, EARLY * TPG)
                    if not (static and i < 1):
                        h_tr(i - 1, (b - 1) % 2)
                    if not (static and i < 2):
                        expert_down(i - 2, b % 2, static and i < 4, expert(i - 2))

            turn(0)
            with pe.Fori(1, TILES // U - 1) as j:
                turn(j)
            turn(TILES // U - 1, last=True)
            pe.wait_ge(eh_ok, TILES - 1)
            gate_up(EARLY * KS, 0, EARLY)
            h_tr(TILES - 1, 1)
            for i in (TILES - 2, TILES - 1):
                expert_down(i, i % 2, False, expert(i))
            pe.wait_ge(eh_ok, TILES)
            for m in range(1, KS):
                gate_up(EARLY * KS + m, m, EARLY)
            pe.wait_ge(ey_ok, TILES)
            downs(EARLY)
            with pe.Fori(EARLY + 1, NG) as g:
                for m in range(KS):
                    gate_up(g * KS + m, m, g)
                downs(g)


def kernel(**inputs):
    import numpy as np
    import concourse.bacc as bacc
    from concourse.bass_utils import run_bass_kernel_spmd

    def lay(a):
        return np.ascontiguousarray(a)

    pre = "L0_cond_"
    x = lay(inputs["x"]).reshape(T, H)
    p = np.arange(P)
    c = np.zeros((P, C_W), np.float32)
    c[:, C_ID:C_ID + P] = np.eye(P)
    c[:, C_TRI:C_TRI + P] = p[:, None] < p[None, :]
    c[:, C_IOTA:C_IOTA + P] = p[None, :]
    c[:, C_REV:C_REV + NE] = NE - np.arange(NE)
    c[:, C_SCAN:C_SCAN + NE * NC] = np.arange(NE * NC) % NC != 0
    c[:, C_TOK:C_TOK + NC] = P * np.arange(NC)[None, :] + p[:, None] - T // 2
    arrays = {
        "x": x, "xT": lay(x.T), "wtT": lay(np.asarray(inputs[pre + "wt"]).T), "wgT": lay(np.asarray(inputs[pre + "wg"]).T),
        "condT": lay(np.asarray(inputs["cond_64"]).T),
        "w_gate": lay(inputs[pre + "w_gate"]), "w_up": lay(inputs[pre + "w_up"]), "w_down": lay(inputs[pre + "w_down"]),
        "sw_gate": lay(inputs[pre + "sw_gate"]), "sw_up": lay(inputs[pre + "sw_up"]), "sw_down": lay(inputs[pre + "sw_down"]),
        "consts": c,
    }
    nc = bacc.Bacc("TRN2", target_bir_lowering=False, num_devices=1)
    arrays = {f"in_{n}": a for n, a in arrays.items()}
    args = [nc.dram_tensor(n, a.shape, mybir.dt.from_np(a.dtype), kind="ExternalInput").ap() for n, a in arrays.items()]
    args.append(nc.dram_tensor("out_dram", (T, H), mybir.dt.float32, kind="ExternalOutput").ap())
    moe_kernel(nc, *args)
    r = run_bass_kernel_spmd(nc, [arrays], core_ids=[0])
    return r.results[0]["out_dram"].reshape(NG, GT, H)
```

```python
import concourse.bass as bass
from concourse import mybir
from contextlib import ExitStack

P = 128
T, H, NE, M, SM, G = 4096, 512, 8, 256, 512, 64
KH = H // P
KM = M // P
KS = SM // P
TOPK = 2
GT = 512
NG = T // GT
TPG = GT // P
NC = T // P
EARLY = 3
U = 4
TILES = T * TOPK // P + NE - 1
TURNS = -(-TILES // U)
LAST = TILES - (TURNS - 1) * U
SLOPE = 0.01
SG, SU, SD, FIRST_E = 0, 1, 2, 3
CHUNKS = FIRST_E + 2 * NE
GU_PART = KH * 2 * M
DN_PART = KM * H
E_SIZE = 2 * (GU_PART + DN_PART)
STEP_CHUNKS = [[], [2], [3], [4], [], [5], [6], [7, 8], [11], [12, 13], [14, 15], [16]]
DOWN_CHUNKS = [[], [9, 10], [17, 18]]
LOADS = [[5, 6, 7, 8], [9, 10, 11, 12, 13], [14, 15, 16, 17, 18]]
ROOM_OF = {5: 2, 6: 3, 7: 4, 8: 5, 9: 6, 10: 7, 11: 8, 12: 9, 13: 10, 15: 11, 16: 13, 17: 12, 18: 15}
HOTS_STEP = 4
MAP_BEHIND = 1
POOL_LEAKY = 2 * KS
C_ID, C_TRI, C_IOTA, C_REV, C_SCAN, C_TOK, C_W = 0, 128, 256, 384, 392, 648, 680


def moe_kernel(nc, x, xT, wtT, wgT, condT, w_gate, w_up, w_down, sw_gate, sw_up, sw_down, consts, out):
    F32, F32R, F16, BF16, I32 = (mybir.dt.float32, mybir.dt.float32r, mybir.dt.float16, mybir.dt.bfloat16,
                                 mybir.dt.int32)
    ALU, ACT, AX = mybir.AluOpType, mybir.ActivationFunctionType, mybir.AxisListType

    xT_v = xT.rearrange("(k p) t -> p k t", p=P)
    wtT_v = wtT.rearrange("(k p) e -> p k e", p=P)
    ctx = ExitStack()
    with ctx:
        def sb(name, shape, dt=F32):
            return ctx.enter_context(nc.sbuf_tensor(name, shape, dt))

        def under(name, shape, dt):
            with nc.sbuf_tensor(name, shape, dt) as t:
                return t

        def sem(name):
            return ctx.enter_context(nc.semaphore(name))

        def sems(name, n):
            return [sem(f"{name}{i}") for i in range(n)]

        WIDE = EARLY
        X_TURN = 1
        assert U == KH
        YW = 2 * TPG
        YB = 4
        slot_rows = nc.dram_tensor("slot_rows", (TILES * P, H), F32, kind="Internal").ap()

        ht_late = under("ht_late", [P, 2, KS, GT], F32R)
        wexp = sb("wexp", [P, NE * E_SIZE // 2])
        wexp16 = wexp[:, :].bitcast(F16)
        swgu = sb("swgu", [P, 2, 2, KH, SM], F16)
        swd = sb("swd", [P, 2, KS, H], F32R)

        def gu_part(e, part):
            at = e * E_SIZE + part * GU_PART
            return wexp16[:, at:at + GU_PART]

        def dn_part(e, part):
            at = e * E_SIZE + 2 * GU_PART + part * DN_PART
            return wexp16[:, at:at + DN_PART]

        cst = sb("cst", [P, C_W])
        tri = sb("tri", [P, P], BF16)
        ones = sb("ones", [P, P], BF16)
        wt_sb = sb("wt_sb", [P, KH, NE])
        wg_sb = sb("wg_sb", [G, NE])
        cond_sb = sb("cond_sb", [G, NG])
        bias_sb = sb("bias_sb", [NE, NG])
        pos = sb("pos", [P, TOPK, NC], I32)
        wts = sb("wts", [P, TOPK, NC])
        slot_tok = sb("slot_tok", [P, TILES], I32)
        tile_exp = sb("tile_exp", [1, TILES], I32)
        tile_f = sb("tile_f", [P, TILES])
        idx_e = sb("idx_e", [P, U], I32)
        idx_c = sb("idx_c", [P, YW, TOPK], I32)
        row_f = sb("row_f", [P, 2 * TOPK, NC])
        squares = sb("squares", [P, CHUNKS + 1])
        sq_all = sb("sq_all", [P, CHUNKS + 1])
        half_exp = sb("half_exp", [P, CHUNKS + 1], I32)
        scale = sb("scale", [P, CHUNKS + 1])
        inv = sb("inv", [P, CHUNKS + 1])
        x_squares = sb("x_squares", [P, NG])
        inv_sh = sb("inv_sh", [P, 3])
        inv_gu = sb("inv_gu", [P, TILES])
        inv_dn = sb("inv_dn", [P, TILES])
        h_sq = sb("h_sq", [P, U])
        h_exp = sb("h_exp", [P, U], I32)
        h_scale = sb("h_scale", [P, U])
        h_inv = sb("h_inv", [P, U])
        y_scale = sb("y_scale", [P, U])
        X = CHUNKS
        acc = sb("acc", [P, EARLY * TPG, H])
        xa = acc[:, (EARLY - 1) * TPG:EARLY * TPG, :]
        xb = sb("xb", [P, KH * GT])
        xhl_early = xb[:, :].bitcast(F16).rearrange("p (s k t) -> p s k t", s=2, k=KH)
        xts = xb[:, 0:1024].bitcast(F16).rearrange("p (b s c) -> p b s c", b=2, s=2)
        he = xb[:, 1024:1536].rearrange("p (b m) -> p b m", b=2)
        hts = xb[:, 1536:2048].bitcast(F16).rearrange("p (b s c) -> p b s c", b=2, s=2)
        gs_t = sb("gs_t", [P, 1024])
        gs = gs_t[:, :].rearrange("p (b t) -> p b t", b=2)
        ge = gs_t[:, 0:512].rearrange("p (b t) -> p b t", b=2)
        lt = gs_t[0:NE, :].rearrange("p (b t) -> p b t", b=2)
        ht_early = under("ht_early", [P, 2, KS, GT], F32R)
        htx = sb("htx", [P, 2 * KS * GT])
        sloped = htx[:, KS * GT:].rearrange("p (m t) -> p m t", m=KS)
        xhl_late = htx[:, 0:2048].bitcast(F16).rearrange("p (s k t) -> p s k t", s=2, k=KH)
        xa_late = htx[:, 2048:4096].rearrange("p (k t) -> p k t", k=KH)
        area1 = sb("area1", [P, 2048])
        area2 = sb("area2", [P, 2048])
        xg = area1[:, :].rearrange("p (b h) -> p b h", b=U)
        z = area1[:, :].rearrange("p (b h) -> p b h", b=TPG)
        ysb = area2[:, :].rearrange("p (b h) -> p b h", b=U)
        yg = wexp[:, 4096:4096 + YB * TOPK * H].rearrange("p (b k h) -> p b k h", b=YB, k=TOPK)

        def flat(v):
            return v.rearrange("p c h -> p (c h)")

        def stage(n):
            if n < 2:
                return flat(acc[:, n * TPG:(n + 1) * TPG, :])
            if n == 14:
                return hot_t[:, 2 * E_SIZE // 2 - DN_PART:2 * E_SIZE // 2]
            if n == 15:
                return area1[:, :]
            if n == 16:
                return hot_t[:, 3 * E_SIZE // 2 - DN_PART:3 * E_SIZE // 2]
            if n == 17:
                return area2[:, :]
            if n == 18:
                return area1[:, 1024:2048]
            return (area1[:, :], area2[:, :], hot_t[:, 3 * E_SIZE // 2 - 2048:3 * E_SIZE // 2])[(n - 2) % 3]

        def x_router(g):
            at = 5 * E_SIZE // 2 + (g - 4) * KH * GT
            return (flat(xa), xb[:, :], htx[:, 0:2048], htx[:, 2048:4096])[g] if g < 4 else wexp[:, at:at + KH * GT]

        def squared(n):
            return [q for q in ((n + 1, n + 2) if n == SD else (n + 2,)) if q < CHUNKS]

        def early(g):
            return isinstance(g, int) and g < EARLY

        scr = wexp[:, 4 * E_SIZE // 2:5 * E_SIZE // 2]
        hot_t = wexp[:, 5 * E_SIZE // 2:]
        hot_row = hot_t[:, 0:4096].bitcast(F16).rearrange("p (k c r) -> p k c r", k=TOPK, c=NC)
        hw = TILES * NC // 2
        hot_v = [hot_t[:, 4096 + k * hw:4096 + (k + 1) * hw].bitcast(F16).rearrange("p (c t) -> p c t", c=NC)
                 for k in range(TOPK)]
        dump = [scr[:, k * 1024:(k + 1) * 1024].bitcast(BF16) for k in range(2)]

        def s3(i):
            return scr[:, i * 256:(i + 1) * 256].rearrange("p (c e) -> p c e", e=NE)

        logit, prob, keep, eq = s3(0), s3(1), s3(2), s3(3)
        hot1, hot2, rank, tmp = s3(4), s3(5), s3(6), s3(7)
        cnt_ec = scr[:, 2048:2304].rearrange("p (e c) -> p e c", e=NE)
        cum_ec = scr[:, 2304:2560].rearrange("p (e c) -> p e c", e=NE)
        small = scr[:, 2560:2880].rearrange("p (n c) -> p n c", n=10)
        etmp = scr[:, 2880:2920].rearrange("p (n e) -> p n e", n=5)
        eint = scr[:, 2920:2928].bitcast(I32)
        row_i = scr[:, 2944:3072].bitcast(I32).rearrange("p (n c) -> p n c", n=2 * TOPK)
        member = sb("member", [P, NC, NE], BF16)
        tile_cmp = sb("tile_cmp", [P, TILES, NE])

        bank = [ctx.enter_context(nc.psum_tensor(f"bank{i}", [P, 512], F32)) for i in range(8)]
        ps_g, ps_u, ps_p = bank[0:2], bank[2:4], bank[4:8]
        ps_x, ps_gu, ps_h, ps_y = bank[0:2], bank[2:4], bank[4:6], bank[6:8]
        ps_lt, ps_bias, ps_log, ps_rank, ps_cnt, ps_map = bank[6:8], bank[4], bank[5], bank[7], bank[6], bank[1]

        wt_in, cst_in = sem("wt_in"), sem("cst_in")
        xt_in = sems("xt_in", NG)
        xa_in = sem("xa_in")
        x1_in = sems("x1_in", KH)
        ch_in = sems("ch_in", 4)
        x_in = sem("x_in")
        cast = sem("cast")
        bias_mm, bias_ok = sem("bias_mm"), sem("bias_ok")
        lt_mm, lt_ok, log_tr = sem("lt_mm"), sem("lt_ok"), sem("log_tr")
        r_step = sem("r_step")
        exp_in, exp_ok = sem("exp_in"), sem("exp_ok")
        member_ok, rank_mm, tokens_ok, route_ok = sem("member_ok"), sem("rank_mm"), sem("tokens_ok"), sem("route_ok")
        counts_ok, rows_ok, hots_ok, map_mm, map_ok = sem("counts_ok"), sem("rows_ok"), sem("hots_ok"), sem("map_mm"), sem("map_ok")
        xsq_act, xsq_dve, xsum_ok, xall_ok, xscale_ok = sem("xsq_act"), sem("xsq_dve"), sem("xsum_ok"), sem("xall_ok"), sem("xscale_ok")
        sq_ok, all_ok, scale_ok, hi_ok, lo_ok = sem("sq_ok"), sem("all_ok"), sem("scale_ok"), sem("hi_ok"), sem("lo_ok")
        xhi_ok, xlo_ok = sem("xhi_ok"), sem("xlo_ok")
        gu_mm, gs_ok, slope_ok, lg_ok, h_ok, hhi_ok, hlo_ok = (sem("gu_mm"), sem("gs_ok"), sem("slope_ok"), sem("lg_ok"), sem("h_ok"),
                                                     sem("hhi_ok"), sem("hlo_ok"))
        p_mm, p_ok = sem("p_mm"), sem("p_ok")
        eidx_ok, xg_in = sem("eidx_ok"), sems("xg_in", U)
        ex_tr, exhi_ok, exlo_ok, eg_mm, eg_ok, elg_ok, eh_ok = (sem("ex_tr"), sem("exhi_ok"), sem("exlo_ok"), sem("eg_mm"),
                                                                sem("eg_ok"), sem("elg_ok"), sem("eh_ok"))
        hsq_ok, hexp_ok, hscale_ok, hinv_ok, yscale_ok, hs_ok = (sem("hsq_ok"), sem("hexp_ok"), sem("hscale_ok"),
                                                                 sem("hinv_ok"), sem("yscale_ok"), sem("hs_ok"))
        eh_tr, ehhi_ok, ehlo_ok, ey_mm, ey_ok, y_out = (sem("eh_tr"), sem("ehhi_ok"), sem("ehlo_ok"), sem("ey_mm"),
                                                        sem("ey_ok"), sems("y_out", U))
        tiles_ok = sem("tiles_ok")
        cidx_ok, yg_in = sem("cidx_ok"), sems("yg_in", YB)
        half_ok, comb_ok = sem("half_ok"), sem("comb_ok")
        z_in, z_out, old_out = sems("z_in", TPG), sems("z_out", TPG), sem("old_out")

        block = ctx.enter_context(nc.Block())
        order = list(range(1, NG)) + [0]

        def chunk_loads(n):
            st = stage(n)
            if n < FIRST_E:
                v = st.rearrange("p (k n) -> p k n", k=KH)
                return [(v, (sw_gate, sw_up, sw_down)[n].rearrange("(k p) n -> p k n", p=P))]
            e = (n - FIRST_E) // 2
            if (n - FIRST_E) % 2:
                return [(st[:, 0:DN_PART].rearrange("p (k n) -> p k n", k=KM), w_down[e].rearrange("(k p) n -> p k n", p=P))]
            v = st.rearrange("p (k n) -> p k n", k=KH)
            return [(v[:, :, 0:M], w_gate[e].rearrange("(k p) n -> p k n", p=P)),
                    (v[:, :, M:2 * M], w_up[e].rearrange("(k p) n -> p k n", p=P))]

        def chunk_arrived(n):
            return 16 * sum(len(chunk_loads(i)) for i in range(n % 4, n + 1, 4))

        def chunk_parts(n):
            st = stage(n)
            if n in (SG, SU):
                return st, swgu[:, n, 0].rearrange("p k n -> p (k n)"), swgu[:, n, 1].rearrange("p k n -> p (k n)")
            if n == SD:
                return st, swd[:, 0].rearrange("p k n -> p (k n)"), swd[:, 1].rearrange("p k n -> p (k n)")
            e = (n - FIRST_E) // 2
            if (n - FIRST_E) % 2:
                return st[:, 0:DN_PART], dn_part(e, 0), dn_part(e, 1)
            return st, gu_part(e, 0), gu_part(e, 1)

        @block.sync
        def _(sp):
            def load_chunk(n):
                if n == 4:
                    sp.wait_ge(lt_mm, NG)
                    sp.wait_ge(xsq_act, NG // 2)
                    sp.wait_ge(xsq_dve, NG // 2)
                if n == 14:
                    sp.wait_ge(map_mm, 1)
                if n in ROOM_OF:
                    sp.wait_ge(hi_ok, ROOM_OF[n] + 1)
                    sp.wait_ge(lo_ok, ROOM_OF[n] + 1)
                for dst, src in chunk_loads(n):
                    sp.dma_start(dst, src).then_inc(ch_in[n % 4], 16)

            sp.dma_start(wt_sb[:, :, :], wtT_v).then_inc(wt_in, 16)
            for j, g in enumerate(order):
                if j == 0:
                    for k in range(KH):
                        sp.dma_start(x_router(g)[:, k * GT:(k + 1) * GT], xT_v[:, k, g * GT:(g + 1) * GT]).then_inc(x1_in[k], 16)
                else:
                    sp.dma_start(x_router(g).rearrange("p (k t) -> p k t", k=KH), xT_v[:, :, g * GT:(g + 1) * GT]
                                 ).then_inc(xt_in[g], 16)
                if j == 0:
                    sp.dma_start(wg_sb[:, :], wgT).then_inc(cst_in, 16)
                    sp.dma_start(cond_sb[:, :], condT).then_inc(cst_in, 16)
                    sp.dma_start(cst[:, :], consts).then_inc(cst_in, 16)
                if j == 1:
                    load_chunk(SG)
                if j == 3:
                    load_chunk(SU)
            load_chunk(SD)
            load_chunk(FIRST_E)
            load_chunk(FIRST_E + 1)
            sp.wait_ge(lo_ok, 2)
            sp.wait_ge(hi_ok, 2)
            for g in range(EARLY):
                if g < EARLY - 1:
                    sp.dma_start(acc[:, g * TPG:(g + 1) * TPG, :],
                                 x[g * GT:(g + 1) * GT, :].rearrange("(c p) h -> p c h", p=P)).then_inc(x_in, 16)
                sp.wait_ge(xhi_ok, g * KH + KH)
                sp.wait_ge(xlo_ok, g * KH + KH)
                if g < EARLY - 1:
                    sp.dma_start(xa, xT_v[:, :, (g + 1) * GT:(g + 2) * GT]).then_inc(xa_in, 16)
                else:
                    sp.dma_start(xa, x[g * GT:(g + 1) * GT, :].rearrange("(c p) h -> p c h", p=P)).then_inc(x_in, 16)
                for n in LOADS[g]:
                    load_chunk(n)
            sp.wait_ge(p_mm, EARLY * TPG)
            sp.dma_start(xa_late, xT_v[:, :, EARLY * GT:(EARLY + 1) * GT]).then_inc(xa_in, 16)
            def store_rows(j, tiles):
                for b in range(tiles):
                    sp.wait_ge(ey_ok, j * U + (b + 1))
                    sp.dma_start(slot_rows[bass.ds((j * U + b) * P, P), :], ysb[:, b, :]).then_inc(y_out[b], 16)

            with sp.Fori(0, TURNS - 1) as j:
                store_rows(j, U)
            store_rows(TURNS - 1, LAST)

            def late(g, first=False, last=False, first_old=None, q0=None):
                for t in range(TPG):
                    if not first:
                        sp.wait_ge(z_out[t], g * 16 - 16 * EARLY)
                    sp.dma_start(z[:, t, :], x[bass.ds((g * TPG + t) * P, P), :]).then_inc(z_in[t], 16)
                if not last:
                    sp.wait_ge(xhi_ok, g * KH + KH)
                    sp.wait_ge(xlo_ok, g * KH + KH)
                    sp.dma_start(xa_late, xT_v[:, :, bass.ds(g * GT + GT, GT)]).then_inc(xa_in, 16)
                if first_old is not None:
                    for o in range(TPG):
                        sp.wait_ge(comb_ok, q0 + 2 * (o + 1))
                        sp.dma_start(out[bass.ds((first_old + o) * P, P), :], acc[:, bass.ds(first_old + o, 1), :]
                                     .rearrange("p o h -> p (o h)")).then_inc(old_out, 16)
                for t in range(TPG):
                    sp.wait_ge(p_ok, g * TPG + (t + 1))
                    sp.dma_start(out[bass.ds((g * TPG + t) * P, P), :], z[:, t, :]).then_inc(z_out[t], 16)

            sp.wait_ge(ex_tr, TILES)
            late(EARLY, first=True, first_old=0, q0=0)
            with sp.Fori(EARLY + 1, EARLY + WIDE) as g:
                late(g, first_old=g * TPG - TPG * EARLY, q0=g * YW - YW * EARLY)
            late(NG - 2)
            late(NG - 1, last=True)
            for t in range(TPG):
                sp.wait_ge(z_out[t], 16 * (NG - EARLY))
            sp.wait_ge(old_out, 16 * EARLY * TPG)

        @block.gpsimd
        def _(pool):
            def times_token(k):
                pool.wait_ge(hots_ok, k + 1)
                nc.gpsimd.tensor_tensor(hot_v[k], hot_v[k], cst[:, C_TOK:C_TOK + NC].unsqueeze(2)
                                        .to_broadcast([P, NC, TILES]), ALU.mult).then_inc(tokens_ok, 1)

            def all_sum(n):
                pool.wait_ge(sq_ok, n + 1)
                nc.gpsimd.partition_all_reduce(sq_all[:, n:n + 1], squares[:, n:n + 1], P, bass.bass_isa.ReduceOp.add).then_inc(all_ok, 1)

            for n in (SG, SU):
                all_sum(n)
            pool.wait_ge(xsum_ok, 1)
            nc.gpsimd.partition_all_reduce(sq_all[:, X:X + 1], squares[:, X:X + 1], P, bass.bass_isa.ReduceOp.add).then_inc(xall_ok, 1)
            def sums(n):
                for q in squared(n):
                    pool.wait_ge(sq_ok, q)
                    nc.gpsimd.partition_all_reduce(sq_all[:, q:q + 1], squares[:, q:q + 1], P,
                                                   bass.bass_isa.ReduceOp.add).then_inc(all_ok, 1)

            def index_x(i, b):
                nc.gpsimd.tensor_copy(idx_e[:, b:b + 1], slot_tok[:, bass.ds(i, 1)]).then_inc(eidx_ok, 1)

            def gather_x(b):
                nc.gpsimd.indirect_dma_start(out=xg[:, b, :], out_offset=None, in_=x,
                                             in_offset=bass.IndirectOffsetOnAxis(ap=idx_e[:, b:b + 1], axis=0)
                                             ).then_inc(xg_in[b], 16)

            def turn_x(j, b):
                i = j * U + b
                pool.wait_ge(ex_tr, i - (U - 2))
                pool.wait_ge(eidx_ok, i + 1)
                index_x(i + 1, (b + 1) % U)
                gather_x(b)

            def first_tiles():
                pool.wait_ge(map_ok, 1)
                index_x(0, 0)
                pool.wait_ge(hi_ok, ROOM_OF[18] + 1)
                pool.wait_ge(lo_ok, ROOM_OF[18] + 1)
                for b in range(2):
                    pool.wait_ge(eidx_ok, b + 1)
                    index_x(b + 1, b + 1)
                    gather_x(b)

            for g in range(EARLY):
                for m in range(KS):
                    s = g * KS + m
                    if s == EARLY * KS - 1:
                        first_tiles()
                    if s < POOL_LEAKY:
                        pool.wait_ge(slope_ok, s + 1)
                        nc.gpsimd.tensor_tensor(gs[:, m % 2, :], gs[:, m % 2, :], sloped[:, m, :], ALU.subtract).then_inc(lg_ok, 1)
                    if HOTS_STEP <= s < HOTS_STEP + TOPK:
                        times_token(s - HOTS_STEP)
                    pool.wait_ge(hhi_ok, s + 1)
                    nc.gpsimd.tensor_tensor(ht_early[:, 1, m, :], gs[:, m % 2, :], ht_early[:, 0, m, :], ALU.subtract
                                            ).then_inc(hlo_ok, 1)
                    for n in STEP_CHUNKS[s]:
                        sums(n)
                for n in DOWN_CHUNKS[g]:
                    sums(n)

            pool.wait_ge(hi_ok, CHUNKS)
            pool.wait_ge(lo_ok, CHUNKS)
            for b in range(2, U - 1):
                pool.wait_ge(eidx_ok, b + 1)
                index_x(b + 1, b + 1)
                gather_x(b)
            turn_x(0, U - 1)
            with pool.Fori(1, TURNS - 1) as j:
                for b in range(U):
                    turn_x(j, b)
            for b in range(LAST - 1):
                turn_x(TURNS - 1, b)
            pool.wait_ge(ex_tr, TILES - U)
            pool.wait_ge(eidx_ok, TILES)
            gather_x(LAST - 1)

            def index_y(c, b):
                nc.gpsimd.tensor_copy(idx_c[:, b, :], pos[:, :, bass.ds(c, 1)].rearrange("p k o -> p (k o)")).then_inc(cidx_ok, 1)

            def gather_y(n, b):
                for k in range(TOPK):
                    nc.gpsimd.indirect_dma_start(out=yg[:, b, k, :], out_offset=None, in_=slot_rows,
                                                 in_offset=bass.IndirectOffsetOnAxis(ap=idx_c[:, n:n + 1, k:k + 1]
                                                                                     .rearrange("p n k -> p (n k)"), axis=0)
                                                 ).then_inc(yg_in[b], 16)

            def turn_y(q, n, c_next):
                if not isinstance(q, int) or q >= YB:
                    pool.wait_ge(comb_ok, q - (YB - 1))
                pool.wait_ge(cidx_ok, q + 1)
                index_y(c_next, (n + 1) % YW)
                gather_y(n, n % YB)

            def wide_order(g, old):
                return [c for t in range(TPG) for c in (g * TPG + t, old + t)] + [g * TPG + TPG]

            index_y(EARLY * TPG, 0)
            for b in range(U):
                pool.wait_ge(y_out[b], 16 * (TURNS - (b >= LAST)))
            tiles = wide_order(EARLY, 0)
            for n in range(YW):
                turn_y(n, n, tiles[n + 1])
            with pool.Fori(EARLY + 1, EARLY + WIDE) as g:
                tiles = wide_order(g, g * TPG - TPG * EARLY)
                for n in range(YW):
                    turn_y(g * YW + (n - YW * EARLY), n, tiles[n + 1])
            q0 = YW * WIDE
            for q in range(q0, NC - 1):
                turn_y(q, q % YW, (EARLY + WIDE) * TPG + q - q0 + 1)
            pool.wait_ge(comb_ok, NC - YB)
            pool.wait_ge(cidx_ok, NC)
            gather_y((NC - 1) % YW, (NC - 1) % YB)

        @block.scalar
        def _(act):
            A, C = nc.scalar.activation, ACT.Copy

            def square(n):
                act.wait_ge(ch_in[n % 4], chunk_arrived(n))
                v, high, _ = chunk_parts(n)
                A(high.bitcast(BF16), v, ACT.Square, accum_out=squares[:, n:n + 1]).then_inc(sq_ok, 1)

            def high(n):
                v, hi, _ = chunk_parts(n)
                if n == SD:
                    act.wait_ge(ch_in[n % 4], chunk_arrived(n))
                    A(hi, v, C).then_inc(hi_ok, 1)
                else:
                    act.wait_ge(scale_ok, n + 1 - (n > SD))
                    A(hi, v, C, scale=scale[:, n:n + 1]).then_inc(hi_ok, 1)

            def squares_behind(n):
                for q in squared(n):
                    if q == FIRST_E + 8:
                        act.wait_ge(route_ok, 1)
                    if q == FIRST_E + 10:
                        act.wait_ge(map_mm, 1)
                    if q in (16, 18):
                        act.wait_ge(lo_ok, q - 1)
                    square(q)

            for j in range(1, NG, 2):
                act.wait_ge(xt_in[order[j]], 16)
                if j > 1:
                    act.wait_ge(xsq_act, j // 2)
                A(dump[0], x_router(order[j]), ACT.Square, accum_out=x_squares[:, j:j + 1]).then_inc(xsq_act, 1)
                if j == 1:
                    act.wait_ge(cst_in, 48)
                    A(tri[:, :], cst[:, C_TRI:C_TRI + P], C)
                    A(ones[:, :], cst[:, C_TRI:C_TRI + P], C, bias=1.0, scale=0.0).then_inc(cast, 1)
                    square(SG)
                if j == 3:
                    square(SU)
                    high(SG)
                if j == 5:
                    high(SU)

            def x_high(g):
                src, dst = (xa, xhl_early) if early(g) else (xa_late, xhl_late)
                if isinstance(g, int) and g == 0:
                    act.wait_ge(xscale_ok, 1)
                    act.wait_ge(lt_mm, order.index(1) + 1)
                else:
                    act.wait_ge(xa_in, g * 16)
                    act.wait_ge(gu_mm, g * KS)
                for k in range(KH):
                    A(dst[:, 0, k, :], src[:, k, :], C, scale=scale[:, X:X + 1]).then_inc(xhi_ok, 1)

            def shared_gate(s, b, first=False):
                act.wait_ge(gu_mm, s + 1)
                if not first:
                    act.wait_ge(hlo_ok, s - 1)
                pool_leaky = isinstance(s, int) and s < POOL_LEAKY
                A(gs[:, b, :], ps_g[b][:, :], ACT.Relu if pool_leaky else C, scale=inv_sh[:, 0:1]).then_inc(gs_ok, 1)
                if pool_leaky:
                    A(sloped[:, s % KS, :], ps_g[b][:, :], ACT.Relu, scale=inv_sh[:, 2:3]).then_inc(slope_ok, 1)

            def h_high(s, m, ht):
                act.wait_ge(h_ok, s + 1)
                A(ht[:, 0, m, :], gs[:, m % 2, :], C).then_inc(hhi_ok, 1)

            x_high(0)
            act.wait_ge(exp_in, 1)
            A(prob, keep, ACT.Exp).then_inc(exp_ok, 1)
            for g in range(EARLY):
                for m in range(KS):
                    s = g * KS + m
                    shared_gate(s, m % 2, first=s < 2)
                    for n in STEP_CHUNKS[s]:
                        high(n)
                    h_high(s, m, ht_early)
                    if m == KS - 1 and g + 1 < EARLY:
                        x_high(g + 1)
                    for n in STEP_CHUNKS[s]:
                        squares_behind(n)
                for n in DOWN_CHUNKS[g]:
                    high(n)
                    squares_behind(n)

            def x_high_e(i, b):
                act.wait_ge(ex_tr, i + 1)
                A(xts[:, b, 0, :], ps_x[b][:, :], C, scale=scale[:, X:X + 1]).then_inc(exhi_ok, 1)

            def gate_out(i, b, first=False):
                act.wait_ge(eg_mm, i + 1)
                if not first:
                    act.wait_ge(hsq_ok, i - 1)
                A(ge[:, b, :], ps_gu[b][:, 0:M], C, scale=inv_gu[:, bass.ds(i, 1)]).then_inc(eg_ok, 1)

            def h_square(i, b, b4):
                act.wait_ge(eh_ok, i + 1)
                A(ge[:, b, :], he[:, b, :], ACT.Square, accum_out=h_sq[:, b4:b4 + 1]).then_inc(hsq_ok, 1)

            def h_high_e(i, b):
                act.wait_ge(eh_tr, i + 1)
                A(hts[:, b, 0, :], ps_h[b][:, 0:M], C).then_inc(ehhi_ok, 1)

            def y_rows(i, b, b4, stored):
                act.wait_ge(ey_mm, i + 1)
                if stored is not None:
                    act.wait_ge(y_out[b4], stored)
                A(ysb[:, b4, :], ps_y[b][:, :], C, scale=y_scale[:, b4:b4 + 1]).then_inc(ey_ok, 1)

            def turn(j, last=False):
                static = isinstance(j, int)
                for b in range(LAST if last else U):
                    i = j * U + b
                    gate_out(i, b % 2, first=static and i < 2)
                    if not (last and b >= LAST - 2):
                        x_high_e(i + 2, b % 2)
                    if not (static and i < 1):
                        h_high_e(i - 1, (b - 1) % 2)
                    h_square(i, b % 2, b)
                    if b >= 2:
                        y_rows(i - 2, b % 2, b - 2, None if static and j == 0 else j * 16)
                    elif not (static and j == 0):
                        y_rows(i - 2, b % 2, b + 2, None if static and j == 1 else j * 16 - 16)
                    if static and j == X_TURN:
                        if b == 0:
                            act.wait_ge(xa_in, EARLY * 16)
                        A(xhl_late[:, 0, b, :], xa_late[:, b, :], C, scale=scale[:, X:X + 1]).then_inc(xhi_ok, 1)

            x_high_e(0, 0)
            x_high_e(1, 1)
            act.wait_ge(tiles_ok, 1)
            turn(0)
            turn(1)
            with act.Fori(2, TURNS - 1) as j:
                turn(j)
            turn(TURNS - 1, last=True)
            h_high_e(TILES - 1, (TILES - 1) % 2)
            for i in (TILES - 2, TILES - 1):
                y_rows(i, i % 2, i % U, 16 * (i // U))

            act.wait_ge(hsq_ok, TILES)
            act.wait_ge(eh_ok, TILES)
            for m in range(KS):
                shared_gate(EARLY * KS + m, m % 2)
                h_high(EARLY * KS + m, m, ht_late)
            with act.Fori(EARLY + 1, NG) as g:
                x_high(g)
                for m in range(KS):
                    shared_gate(g * KS + m, m % 2)
                    h_high(g * KS + m, m, ht_late)

        @block.vector
        def _(dve):
            step = [0]

            def then(ins):
                step[0] += 1
                ins.then_inc(r_step, 1)
                dve.wait_ge(r_step, step[0])

            def bc(v):
                return v.unsqueeze(2).to_broadcast([P, NC, NE])

            V = nc.vector
            TWO23 = float(1 << 23)

            def power(sq, ex, sc, iv):
                then(V.tensor_scalar(ex, sq.bitcast(I32), 24, None, ALU.logical_shift_right))
                V.tensor_scalar(sc.bitcast(I32), ex, -TWO23, 204 * TWO23, ALU.mult, ALU.add)
                return V.tensor_scalar(iv.bitcast(I32), ex, TWO23, 50 * TWO23, ALU.mult, ALU.add)

            def chunk_scale(n):
                dve.wait_ge(all_ok, n + 1 - (n > SD))
                c = slice(n, n + 1)
                power(sq_all[:, c], half_exp[:, c], scale[:, c], inv[:, c]).then_inc(scale_ok, 1)

            def chunk_low(n):
                v, hi, lo = chunk_parts(n)
                dve.wait_ge(hi_ok, n + 1)
                if n == SD:
                    V.tensor_tensor(lo, v, hi, ALU.subtract).then_inc(lo_ok, 1)
                else:
                    V.scalar_tensor_tensor(lo, v, scale[:, n:n + 1], hi, ALU.mult, ALU.subtract).then_inc(lo_ok, 1)

            def x_scale():
                dve.wait_ge(xsq_act, NG // 2)
                dve.wait_ge(xsq_dve, NG // 2)
                V.tensor_reduce(squares[:, X:X + 1], x_squares[:, :], AX.X, ALU.add).then_inc(xsum_ok, 1)
                dve.wait_ge(xall_ok, 1)
                then(power(sq_all[:, X:X + 1], half_exp[:, X:X + 1], scale[:, X:X + 1], inv[:, X:X + 1]))
                then(V.tensor_scalar(inv_sh[:, 0:2], inv[:, SG:SU + 1], inv[:, X:X + 1], None, ALU.mult))
                V.tensor_scalar(inv_sh[:, 2:3], inv_sh[:, 0:1], -SLOPE, None, ALU.mult).then_inc(xscale_ok, 1)

            for j, g in enumerate(order):
                if j % 2 == 0:
                    if j:
                        dve.wait_ge(xt_in[g], 16)
                        dve.wait_ge(xsq_dve, j // 2)
                    else:
                        for k in range(KH):
                            dve.wait_ge(x1_in[k], 16)
                    V.scalar_tensor_tensor(dump[1], x_router(g), 1.0, x_router(g), ALU.mult, ALU.mult,
                                           accum_out=x_squares[:, j:j + 1]).then_inc(xsq_dve, 1)
                if j == 0:
                    dve.wait_ge(bias_mm, 1)
                    V.tensor_copy(bias_sb[:, :], ps_bias[0:NE, 0:NG]).then_inc(bias_ok, 1)
                    dve.wait_ge(bias_ok, 1)
                if j == NG - 1:
                    x_scale()
                dve.wait_ge(lt_mm, j + 1)
                if j >= 2:
                    dve.wait_ge(log_tr, j - 1)
                V.tensor_scalar(lt[:, j % 2, :], ps_lt[j % 2][0:NE, :], bias_sb[:, g:g + 1], 0.5,
                                ALU.add, ALU.mult).then_inc(lt_ok, 1)
                if j == 1:
                    chunk_scale(SG)
                if j == 3:
                    chunk_scale(SU)
                    chunk_low(SG)
                if j == 5:
                    chunk_low(SU)
            def x_low(g):
                src, dst = (xa, xhl_early) if early(g) else (xa_late, xhl_late)
                for k in range(KH):
                    dve.wait_ge(xhi_ok, g * KH + (k + 1))
                    V.scalar_tensor_tensor(dst[:, 1, k, :], src[:, k, :], scale[:, X:X + 1], dst[:, 0, k, :],
                                           ALU.mult, ALU.subtract).then_inc(xlo_ok, 1)

            mx, den, m1, m2, r1, r2, wsum = (small[:, i] for i in range(7))
            x_low(0)
            dve.wait_ge(log_tr, NG)
            then(V.tensor_copy(logit, ps_log[:, 0:NC * NE].rearrange("p (c e) -> p c e", e=NE)))
            then(V.tensor_reduce(mx, logit, AX.X, ALU.max))
            V.tensor_tensor(keep, logit, bc(mx), ALU.subtract).then_inc(exp_in, 1)
            dve.wait_ge(exp_ok, 1)
            then(V.tensor_reduce(den, prob, AX.X, ALU.add))
            then(V.reciprocal(den, den))
            then(V.tensor_tensor(prob, prob, bc(den), ALU.mult))
            rev = cst[:, C_REV:C_REV + NE].unsqueeze(1).to_broadcast([P, NC, NE])
            then(V.tensor_reduce(m1, prob, AX.X, ALU.max))
            then(V.tensor_tensor(eq, prob, bc(m1), ALU.is_equal))
            then(V.tensor_tensor(eq, eq, rev, ALU.mult))
            then(V.tensor_reduce(r1, eq, AX.X, ALU.max))
            then(V.tensor_tensor(hot1, rev, bc(r1), ALU.is_equal))

            def second_choice():
                then(V.scalar_tensor_tensor(keep, hot1, -2.0, prob, ALU.mult, ALU.add))
                then(V.tensor_reduce(m2, keep, AX.X, ALU.max))
                then(V.tensor_tensor(eq, keep, bc(m2), ALU.is_equal))
                then(V.tensor_tensor(eq, eq, rev, ALU.mult))
                then(V.tensor_reduce(r2, eq, AX.X, ALU.max))
                then(V.tensor_tensor(hot2, rev, bc(r2), ALU.is_equal))
                V.tensor_tensor(member[:, :, :], hot1, hot2, ALU.add).then_inc(member_ok, 1)

            end = etmp[:, 2]

            def weights():
                then(V.tensor_tensor(wsum, m1, m2, ALU.add))
                then(V.tensor_scalar(wsum, wsum, 1e-20, None, ALU.add))
                then(V.reciprocal(wsum, wsum))
                V.tensor_tensor(wts[:, 0, :], m1, wsum, ALU.mult)
                V.tensor_tensor(wts[:, 1, :], m2, wsum, ALU.mult)

            def counts():
                dve.wait_ge(rank_mm, 1)
                V.tensor_copy(rank, ps_rank[:, 0:NC * NE].rearrange("p (c e) -> p c e", e=NE))
                V.tensor_copy(cnt_ec, ps_cnt[:, 0:NC * NE].rearrange("p (c e) -> p e c", e=NE)).then_inc(counts_ok, 1)
                dve.wait_ge(counts_ok, 1)

            def positions():
                cnt_f = cnt_ec.rearrange("p e c -> p (e c)")
                cum_f = cum_ec.rearrange("p e c -> p (e c)")
                then(V.tensor_tensor_scan(cum_f, cst[:, C_SCAN:C_SCAN + NE * NC], cnt_f, 0.0, ALU.mult, ALU.add))
                then(V.tensor_tensor(cnt_ec, cum_ec, cnt_ec, ALU.subtract))
                then(V.tensor_tensor(rank, rank, cnt_ec.rearrange("p e c -> p c e"), ALU.add))

            def tiles_of_experts():
                tot, tiles, _, base, one = (etmp[:, i] for i in range(5))
                then(V.tensor_scalar(tot, cum_ec[:, :, NC - 1], float(P - 1), None, ALU.add))
                then(V.tensor_copy(eint, tot))
                then(V.tensor_scalar(eint, eint, 7, None, ALU.logical_shift_right))
                then(V.tensor_copy(tiles, eint))
                then(V.memset(one, 1.0))
                then(V.tensor_tensor_scan(end, one, tiles, 0.0, ALU.mult, ALU.add))
                then(V.tensor_tensor(base, end, tiles, ALU.subtract))
                then(V.tensor_scalar(base, base, float(P), None, ALU.mult))
                then(V.tensor_tensor(rank, rank, base.unsqueeze(1).to_broadcast([P, NC, NE]), ALU.add))

            def slots():
                for k, hot in enumerate((hot1, hot2)):
                    then(V.tensor_tensor(tmp, hot, rank, ALU.mult))
                    then(V.tensor_reduce(small[:, 8 + k], tmp, AX.X, ALU.add))
                then(V.tensor_copy(pos[:, :, :], small[:, 8:10, :]))
                V.tensor_scalar(row_i[:, 0:TOPK, :], pos[:, :, :], P - 1, None, ALU.bitwise_and)
                then(V.tensor_scalar(row_i[:, TOPK:2 * TOPK, :], pos[:, :, :], 7, None, ALU.logical_shift_right))
                then(V.tensor_copy(row_f[:, :, :], row_i[:, :, :]))
                tb = [P, TILES, NE]
                then(V.tensor_tensor(tile_cmp[:, :, :], end.unsqueeze(1).to_broadcast(tb),
                                     cst[:, C_IOTA:C_IOTA + TILES].unsqueeze(2).to_broadcast(tb), ALU.is_le))
                then(V.tensor_reduce(tile_f[:, :], tile_cmp[:, :, :], AX.X, ALU.add))
                then(V.tensor_scalar(tile_f[:, :], tile_f[:, :], float(NE - 1), None, ALU.min))
                V.tensor_copy(tile_exp[:, :], tile_f[0:1, :]).then_inc(route_ok, 1)

            def tile_hots():
                tb = [P, TILES, NE]
                then(V.tensor_tensor(tile_cmp[:, :, :], cst[:, C_IOTA:C_IOTA + NE].unsqueeze(1).to_broadcast(tb),
                                     tile_f[:, :].unsqueeze(2).to_broadcast(tb), ALU.is_equal))

            def tile_scales(down):
                tb = [P, TILES, NE]
                prod = gs_t[:, 0:TILES * NE].rearrange("p (t e) -> p t e", e=NE)
                dve.wait_ge(hlo_ok, EARLY * KS)
                src, dst = inv[:, FIRST_E + down:CHUNKS:2], (inv_gu, inv_dn)[down]
                dve.wait_ge(scale_ok, CHUNKS - 2 + down)
                then(V.tensor_tensor(prod, tile_cmp[:, :, :], src.unsqueeze(1).to_broadcast(tb), ALU.mult))
                then(V.tensor_reduce(dst[:, :], prod, AX.X, ALU.add))
                if not down:
                    V.tensor_scalar(inv_gu[:, :], inv_gu[:, :], inv[:, X:X + 1], None, ALU.mult).then_inc(tiles_ok, 1)

            def hot_tiles(k):
                V.tensor_tensor(hot_v[k], cst[:, C_IOTA:C_IOTA + TILES].unsqueeze(1).to_broadcast([P, NC, TILES]),
                                row_f[:, TOPK + k].unsqueeze(2).to_broadcast([P, NC, TILES]), ALU.is_equal
                                ).then_inc(hots_ok, 1)

            def hot_rows(k):
                V.tensor_tensor(hot_row[:, k], cst[:, C_IOTA:C_IOTA + P].unsqueeze(1).to_broadcast([P, NC, P]),
                                row_f[:, k].unsqueeze(2).to_broadcast([P, NC, P]), ALU.is_equal).then_inc(rows_ok, 1)

            def shared_h(s, m, ht, chunks=()):
                b = m % 2
                g = gs[:, b, :]
                if not (isinstance(s, int) and s < POOL_LEAKY):
                    dve.wait_ge(gs_ok, s + 1)
                    V.scalar_tensor_tensor(g, g, SLOPE, g, ALU.mult, ALU.max).then_inc(lg_ok, 1)
                dve.wait_ge(lg_ok, s + 1)
                V.scalar_tensor_tensor(g, ps_u[b][:, :], inv_sh[:, 1:2], g, ALU.mult, ALU.mult).then_inc(h_ok, 1)
                for n in chunks:
                    chunk_low(n)
                if ht is ht_late:
                    dve.wait_ge(hhi_ok, s + 1)
                    V.tensor_tensor(ht[:, 1, m, :], g, ht[:, 0, m, :], ALU.subtract).then_inc(hlo_ok, 1)

            def add_p(rows, g, t):
                dve.wait_ge(p_mm, g * TPG + (t + 1))
                V.tensor_tensor(rows, ps_p[t][:, :], rows, ALU.add).then_inc(p_ok, 1)

            def scales(chunks):
                for n in chunks:
                    if n != SD:
                        chunk_scale(n)

            def adds(g):
                dve.wait_ge(x_in, 16 * (g + 1))
                for t in range(TPG):
                    add_p(acc[:, g * TPG + t, :], g, t)

            behind = {0: [second_choice], 1: [weights], 4: [lambda: hot_tiles(1)], 5: [lambda: adds(0), lambda: hot_rows(0)], 6: [lambda: hot_rows(1)],
                      2 * KS + 1: [lambda: adds(1)], 3 * KS - 1: [tile_hots]}
            for g in range(EARLY):
                for m in range(KS):
                    s = g * KS + m
                    if s == 2:
                        counts()
                    scales(STEP_CHUNKS[s])
                    shared_h(s, m, ht_early, STEP_CHUNKS[s])
                    for part in behind.get(s, ()):
                        part()
                if g + 1 < EARLY:
                    x_low(g + 1)
                if g == 0:
                    positions()
                    tiles_of_experts()
                    slots()
                    hot_tiles(0)
                chunks = DOWN_CHUNKS[g]
                scales(chunks[:1])
                for i, n in enumerate(chunks):
                    if n == CHUNKS - 2:
                        tile_scales(0)
                    scales(chunks[i + 1:i + 2])
                    if n == CHUNKS - 2:
                        tile_scales(1)
                    if g == 1 and i == MAP_BEHIND:
                        dve.wait_ge(map_mm, 1)
                        V.tensor_scalar(slot_tok[:, :], ps_map[:, 0:TILES], float(T // 2), None, ALU.add).then_inc(map_ok, 1)
                    chunk_low(n)
            dve.wait_ge(tiles_ok, 1)

            def expert_h(i, b, b4, first, last=False):
                g, h = ge[:, b, :], he[:, b, :]
                dve.wait_ge(eg_ok, i + 1)
                V.scalar_tensor_tensor(g, g, SLOPE, g, ALU.mult, ALU.max).then_inc(elg_ok, 1)
                dve.wait_ge(elg_ok, i + 1)
                if not first:
                    dve.wait_ge(eh_tr, i - 1)
                V.scalar_tensor_tensor(h, ps_gu[b][:, M:2 * M], inv_gu[:, bass.ds(i, 1)], g, ALU.mult, ALU.mult
                                       ).then_inc(eh_ok, 1)
                if not last:
                    x_low_e(i + 2, b)
                c = slice(b4, b4 + 1)
                dve.wait_ge(hsq_ok, i + 1)
                V.tensor_scalar(h_exp[:, c], h_sq[:, c].bitcast(I32), 24, None, ALU.logical_shift_right).then_inc(hexp_ok, 1)
                dve.wait_ge(hexp_ok, i + 1)
                V.tensor_scalar(h_scale[:, c].bitcast(I32), h_exp[:, c], -TWO23, 204 * TWO23, ALU.mult, ALU.add
                                ).then_inc(hscale_ok, 1)
                V.tensor_scalar(h_inv[:, c].bitcast(I32), h_exp[:, c], TWO23, 50 * TWO23, ALU.mult, ALU.add
                                ).then_inc(hinv_ok, 1)
                dve.wait_ge(hscale_ok, i + 1)
                V.tensor_scalar(h, h, h_scale[:, c], None, ALU.mult).then_inc(hs_ok, 1)
                dve.wait_ge(hinv_ok, i + 1)
                V.tensor_tensor(y_scale[:, c], h_inv[:, c], inv_dn[:, bass.ds(i, 1)], ALU.mult).then_inc(yscale_ok, 1)

            def x_low_e(i, b):
                dve.wait_ge(exhi_ok, i + 1)
                V.scalar_tensor_tensor(xts[:, b, 1, :], ps_x[b][:, :], scale[:, X:X + 1], xts[:, b, 0, :],
                                       ALU.mult, ALU.subtract).then_inc(exlo_ok, 1)

            def h_low_e(i, b):
                dve.wait_ge(ehhi_ok, i + 1)
                V.tensor_tensor(hts[:, b, 1, :], ps_h[b][:, 0:M], hts[:, b, 0, :], ALU.subtract).then_inc(ehlo_ok, 1)

            x_low_e(0, 0)
            x_low_e(1, 1)
            adds(EARLY - 1)
            for i in range(U * (X_TURN + 1)):
                b = i % U
                if i >= U:
                    dve.wait_ge(ey_ok, i - 3)
                expert_h(i, b % 2, b, i < 2)
                if i >= 1:
                    h_low_e(i - 1, (b - 1) % 2)
                if i >= U * X_TURN:
                    dve.wait_ge(xhi_ok, EARLY * KH + b + 1)
                    V.scalar_tensor_tensor(xhl_late[:, 1, b, :], xa_late[:, b, :], scale[:, X:X + 1], xhl_late[:, 0, b, :],
                                           ALU.mult, ALU.subtract).then_inc(xlo_ok, 1)
            with dve.Fori(X_TURN + 1, TURNS - 1) as j:
                for b in range(U):
                    dve.wait_ge(ey_ok, j * U + (b - 3))
                    expert_h(j * U + b, b % 2, b, False)
                    h_low_e(j * U + (b - 1), (b - 1) % 2)
            for b in range(LAST):
                i = TILES - LAST + b
                dve.wait_ge(ey_ok, i - 3)
                expert_h(i, b % 2, b, False, last=b >= LAST - 2)
                h_low_e(i - 1, (b - 1) % 2)
            h_low_e(TILES - 1, (TILES - 1) % 2)

            def combine(rows, c, q, b, turns):
                dve.wait_ge(yg_in[b], turns * 32)
                V.scalar_tensor_tensor(rows, yg[:, b, 0, :], wts[:, 0, bass.ds(c, 1)], rows, ALU.mult, ALU.add
                                       ).then_inc(half_ok, 1)
                dve.wait_ge(half_ok, q + 1)
                return V.scalar_tensor_tensor(rows, yg[:, b, 1, :], wts[:, 1, bass.ds(c, 1)], rows, ALU.mult, ALU.add
                                              ).then_inc(comb_ok, 1)

            def late(g, q0, first_old=None):
                per = 2 if first_old is not None else 1
                n = 0
                for m in range(KS):
                    shared_h(g * KS + m, m, ht_late)
                    if m == KS - 1 and not (isinstance(g, int) and g == NG - 1):
                        x_low(g + 1)
                    for _ in range((0, per, per, 2 * per)[m]):
                        t = n // per
                        q = q0 + n
                        turns = q // YB + 1 if isinstance(q, int) else g * (YW // YB) + (n // YB + 1 - EARLY * YW // YB)
                        if n % per == 0:
                            dve.wait_ge(z_in[t], g * 16 - 16 * (EARLY - 1))
                            combine(z[:, t, :], g * TPG + t, q, n % YB, turns)
                        else:
                            row = acc[:, bass.ds(first_old + t, 1), :].rearrange("p o h -> p (o h)")
                            combine(row, first_old + t, q, n % YB, turns)
                        n += 1
                for t in range(TPG):
                    dve.wait_ge(comb_ok, q0 + n)
                    add_p(z[:, t, :], g, t)

            late(EARLY, 0, first_old=0)
            with dve.Fori(EARLY + 1, EARLY + WIDE) as g:
                late(g, g * YW - YW * EARLY, first_old=g * TPG - TPG * EARLY)
            late(NG - 2, YW * WIDE)
            late(NG - 1, YW * WIDE + TPG)

        @block.tensor
        def _(pe):
            mm = nc.tensor.matmul
            ident = cst[:, C_ID:C_ID + P]
            PASSES = ((0, 0), (0, 1), (1, 0))
            pe.wait_ge(wt_in, 16)

            def logits_tr(j):
                pe.wait_ge(lt_ok, j + 1)
                for t in range(TPG):
                    c = order[j] * TPG + t
                    last = nc.tensor.transpose(ps_log[:, c * NE:(c + 1) * NE], lt[:, j % 2, t * P:(t + 1) * P],
                                               ident[0:NE, 0:NE])
                last.then_inc(log_tr, 1)

            for j, g in enumerate(order):
                if j:
                    pe.wait_ge(xt_in[g], 16)
                if j >= 2:
                    pe.wait_ge(lt_ok, j - 1)
                for k in range(KH):
                    if j == 0:
                        pe.wait_ge(x1_in[k], 16)
                    last = mm(ps_lt[j % 2][0:NE, :], wt_sb[:, k, :], x_router(g)[:, k * GT:(k + 1) * GT],
                              start=k == 0, stop=k == KH - 1)
                last.then_inc(lt_mm, 1)
                if j == 0:
                    pe.wait_ge(cst_in, 48)
                    mm(ps_bias[0:NE, 0:NG], wg_sb[:, :], cond_sb[:, :], start=True, stop=True).then_inc(bias_mm, 1)
                if j >= 1:
                    logits_tr(j - 1)
            logits_tr(NG - 1)

            def gate_up(s, m, g, first=False):
                b = m % 2
                xhl = xhl_early if early(g) else xhl_late
                if not first:
                    pe.wait_ge(h_ok, s - 1)
                for which, ps in ((0, ps_g), (1, ps_u)):
                    n = 0
                    for k in range(KH):
                        if m == 0 and which == 0:
                            pe.wait_ge(xlo_ok, g * KH + (k + 1))
                        for wp, xp in PASSES:
                            last = mm(ps[b][:, :], swgu[:, which, wp, k, m * P:(m + 1) * P], xhl[:, xp, k, :],
                                      start=n == 0, stop=n == 3 * KH - 1)
                            n += 1
                last.then_inc(gu_mm, 1)

            def down(g, ahead_of_last=None):
                ht = ht_early if early(g) else ht_late
                for m in range(KS):
                    if m == KS - 1 and ahead_of_last is not None:
                        ahead_of_last()
                    pe.wait_ge(hlo_ok, g * KS + (m + 1))
                    for t in range(TPG):
                        if m == 0 and not (early(g) and g == 0):
                            pe.wait_ge(p_ok, g * TPG + (t + 1 - TPG))
                        if m == 0 and t == 2 and early(g) and g == 0:
                            pe.wait_ge(counts_ok, 1)
                        for n, (hp, wp) in enumerate(PASSES):
                            last = mm(ps_p[t][:, :], ht[:, hp, m, t * P:(t + 1) * P], swd[:, wp, m, :],
                                      start=m == 0 and n == 0, stop=m == KS - 1 and n == 2)
                        if m == KS - 1:
                            last.then_inc(p_mm, 1)

            def slot_map():
                pe.wait_ge(rows_ok, TOPK)
                pe.wait_ge(tokens_ok, TOPK)
                pe.wait_ge(h_ok, 2 * KS)
                n = 0
                for k in range(TOPK):
                    for c in range(NC):
                        last = mm(ps_map[:, 0:TILES], hot_row[:, k, c, :], hot_v[k][:, c, :],
                                  start=n == 0, stop=n == TOPK * NC - 1)
                        n += 1
                last.then_inc(map_mm, 1)

            pe.wait_ge(lo_ok, 2)
            for g in range(EARLY):
                for m in range(KS):
                    s = g * KS + m
                    if s == 2 * KS + 1:
                        pe.wait_ge(map_ok, 1)
                    gate_up(s, m, g, first=s < 2)
                    if s == 2:
                        pe.wait_ge(cast, 1)
                        pe.wait_ge(member_ok, 1)
                        mem = member[:, :, :].rearrange("p c e -> p (c e)")
                        mm(ps_rank[:, 0:NC * NE], tri[:, :], mem, start=True, stop=True)
                        mm(ps_cnt[:, 0:NC * NE], ones[:, :], mem, start=True, stop=True).then_inc(rank_mm, 1)
                if g == 0:
                    pe.wait_ge(lo_ok, SD + 1)
                down(g, slot_map if g == 1 else None)

            def x_tr(i, b, b4, turn):
                pe.wait_ge(xg_in[b4], turn)
                for k in range(KH):
                    last = nc.tensor.transpose(ps_x[b][:, k * P:(k + 1) * P], xg[:, b4, k * P:(k + 1) * P], ident)
                last.then_inc(ex_tr, 1)

            def expert_gate_up(i, b, first, e):
                pe.wait_ge(exlo_ok, i + 1)
                if not first:
                    pe.wait_ge(eh_ok, i - 1)
                n = 0
                for wp in range(2):
                    for k in range(KH):
                        w = wexp16[:, bass.ds(e * E_SIZE + (wp * GU_PART + k * 2 * M), 2 * M)]
                        for xp in range(2 - wp):
                            last = mm(ps_gu[b][:, :], xts[:, b, xp, k * P:(k + 1) * P], w, start=n == 0, stop=n == 3 * KH - 1)
                            n += 1
                last.then_inc(eg_mm, 1)

            def h_tr(i, b):
                pe.wait_ge(hs_ok, i + 1)
                for m in range(KM):
                    last = nc.tensor.transpose(ps_h[b][:, m * P:(m + 1) * P], he[:, b, m * P:(m + 1) * P], ident)
                last.then_inc(eh_tr, 1)

            def expert_down(i, b, first, e):
                pe.wait_ge(ehlo_ok, i + 1)
                pe.wait_ge(yscale_ok, i + 1)
                if not first:
                    pe.wait_ge(ey_ok, i - 1)
                n = 0
                for wp in range(2):
                    for m in range(KM):
                        w = wexp16[:, bass.ds(e * E_SIZE + (2 * GU_PART + wp * DN_PART + m * H), H)]
                        for hp in range(2 - wp):
                            last = mm(ps_y[b][:, :], hts[:, b, hp, m * P:(m + 1) * P], w, start=n == 0, stop=n == 3 * KM - 1)
                            n += 1
                last.then_inc(ey_mm, 1)

            def expert(i):
                return nc.tensor.value_load(tile_exp[0:1, bass.ds(i, 1)], min_val=0, max_val=NE - 1)

            pe.wait_ge(route_ok, 1)
            x_tr(0, 0, 0, 16)
            x_tr(1, 1, 1, 16)

            def turn(j, last=False):
                static = isinstance(j, int)
                for b in range(LAST if last else U):
                    i = j * U + b
                    expert_gate_up(i, b % 2, static and i < 2, expert(i))
                    if not (last and b >= LAST - 2):
                        x_tr(i + 2, b % 2, (b + 2) % U, j * 16 + (16 if b < U - 2 else 32))
                    if static and i == 1:
                        pe.wait_ge(p_ok, EARLY * TPG)
                    if not (static and i < 1):
                        h_tr(i - 1, (b - 1) % 2)
                    if not (static and i < 2):
                        expert_down(i - 2, b % 2, static and i < 4, expert(i - 2))

            turn(0)
            with pe.Fori(1, TURNS - 1) as j:
                turn(j)
            turn(TURNS - 1, last=True)
            pe.wait_ge(eh_ok, TILES)
            gate_up(EARLY * KS, 0, EARLY)
            h_tr(TILES - 1, (TILES - 1) % 2)
            for i in (TILES - 2, TILES - 1):
                expert_down(i, i % 2, False, expert(i))
            for m in range(1, KS):
                gate_up(EARLY * KS + m, m, EARLY)
            pe.wait_ge(ey_ok, TILES)
            down(EARLY)
            with pe.Fori(EARLY + 1, NG) as g:
                for m in range(KS):
                    gate_up(g * KS + m, m, g)
                down(g)


def kernel(**inputs):
    import numpy as np
    import concourse.bacc as bacc
    from concourse.bass_utils import run_bass_kernel_spmd

    def lay(a):
        return np.ascontiguousarray(a)

    pre = "L0_cond_"
    x = lay(inputs["x"]).reshape(T, H)
    p = np.arange(P)
    c = np.zeros((P, C_W), np.float32)
    c[:, C_ID:C_ID + P] = np.eye(P)
    c[:, C_TRI:C_TRI + P] = p[:, None] < p[None, :]
    c[:, C_IOTA:C_IOTA + P] = p[None, :]
    c[:, C_REV:C_REV + NE] = NE - np.arange(NE)
    c[:, C_SCAN:C_SCAN + NE * NC] = np.arange(NE * NC) % NC != 0
    c[:, C_TOK:C_TOK + NC] = P * np.arange(NC)[None, :] + p[:, None] - T // 2
    arrays = {
        "x": x, "xT": lay(x.T), "wtT": lay(np.asarray(inputs[pre + "wt"]).T), "wgT": lay(np.asarray(inputs[pre + "wg"]).T),
        "condT": lay(np.asarray(inputs["cond_64"]).T),
        "w_gate": lay(inputs[pre + "w_gate"]), "w_up": lay(inputs[pre + "w_up"]), "w_down": lay(inputs[pre + "w_down"]),
        "sw_gate": lay(inputs[pre + "sw_gate"]), "sw_up": lay(inputs[pre + "sw_up"]), "sw_down": lay(inputs[pre + "sw_down"]),
        "consts": c,
    }
    nc = bacc.Bacc("TRN2", target_bir_lowering=False, num_devices=1)
    arrays = {f"in_{n}": a for n, a in arrays.items()}
    args = [nc.dram_tensor(n, a.shape, mybir.dt.from_np(a.dtype), kind="ExternalInput").ap() for n, a in arrays.items()]
    args.append(nc.dram_tensor("out_dram", (T, H), mybir.dt.float32, kind="ExternalOutput").ap())
    moe_kernel(nc, *args)
    r = run_bass_kernel_spmd(nc, [arrays], core_ids=[0])
    return r.results[0]["out_dram"].reshape(NG, GT, H)
```
